# Optimizing a Trainium2 kernel written in Bass

```python
import numpy as np
import jax
import jax.numpy as jnp

def _softmax(x, axis=-1):
    return jax.nn.softmax(x, axis=axis)

def _gelu(x):
    return jax.nn.gelu(x, approximate=True)

def _silu(x):
    return jax.nn.silu(x)

def _sigmoid(x):
    return jax.nn.sigmoid(x)

def _layernorm(x, axis=-1, eps=1e-05):
    m = jnp.mean(x, axis=axis, keepdims=True)
    v = jnp.var(x, axis=axis, keepdims=True)
    return (x - m) / jnp.sqrt(v + eps)

def _scatter_add(tgt, idx, src, axis=0):
    return tgt.at[idx].add(src)

def _segment_sum(src, seg, n):
    return jax.ops.segment_sum(src, seg, n)
kernel_name = 'mk_conv_preact_d1_conv_nchw128_r4_7ad01b'

def setup_inputs(seed: int=0):
    np.random.seed(seed)
    _w = jnp.asarray

    def _rec_inputs():
        import jax
        import jax.numpy as jnp
        _gk = jax.random.key(seed)
        x = -3.91e-05 + 0.9999 * jax.random.normal(jax.random.fold_in(_gk, 1), (32, 32, 110, 110), jnp.float32)
        return x
    x = _rec_inputs()

    def _L0_conv_setup():
        import jax, jax.numpy as jnp
        import numpy as np
        C = 32
        H = 110
        K = 192
        NH = 8
        EPS_BN = 1e-05
        EPS_LN = 1e-05

        def make_pos(seq_len, dim):
            pos = np.arange(seq_len, dtype=np.float32)[:, None]
            div = np.exp(np.arange(0, dim, 2, dtype=np.float32) * -(np.log(10000.0) / dim))
            pe = np.zeros((seq_len, dim), dtype=np.float32)
            pe[:, 0::2] = np.sin(pos * div)
            pe[:, 1::2] = np.cos(pos * div)
            return jnp.asarray(pe)

        def _layernorm(t, g, b):
            mu = t.mean(-1, keepdims=True)
            var = t.var(-1, keepdims=True)
            return (t - mu) / jnp.sqrt(var + EPS_LN) * g + b
        key = jax.random.key(seed)
        ks = jax.random.split(key, 10)
        B = 32
        s = 0.05
        return {'x': jax.random.normal(ks[0], (B, C, H, H), jnp.float32), 'conv_w': jax.random.normal(ks[1], (1, C, 7, 7), jnp.float32) * s, 'conv_b': jnp.zeros((1,), jnp.float32), 'bn_g': jnp.ones((1,), jnp.float32), 'bn_b': jnp.zeros((1,), jnp.float32), 'bn_m': jnp.zeros((1,), jnp.float32), 'bn_v': jnp.ones((1,), jnp.float32), 'w_qkv': jax.random.normal(ks[2], (3 * C, C), jnp.float32) * s, 'b_qkv': jnp.zeros((3 * C,), jnp.float32), 'w_o': jax.random.normal(ks[3], (C, C), jnp.float32) * s, 'b_o': jnp.zeros((C,), jnp.float32), 'ln1_g': jnp.ones((C,), jnp.float32), 'ln1_b': jnp.zeros((C,), jnp.float32), 'w1': jax.random.normal(ks[4], (2 * C, C), jnp.float32) * s, 'b1': jnp.zeros((2 * C,), jnp.float32), 'w2': jax.random.normal(ks[5], (C, 2 * C), jnp.float32) * s, 'b2': jnp.zeros((C,), jnp.float32), 'ln2_g': jnp.ones((C,), jnp.float32), 'ln2_b': jnp.zeros((C,), jnp.float32)}
    _L0_conv_all = _L0_conv_setup()
    _L0_conv_in = {k: v for k, v in _L0_conv_all.items() if k in ('conv_w', 'conv_b', 'bn_g', 'bn_b', 'bn_m', 'bn_v', 'w_qkv', 'b_qkv', 'w_o', 'b_o', 'ln1_g', 'ln1_b', 'w1', 'b1', 'w2', 'b2', 'ln2_g', 'ln2_b')}
    del _L0_conv_all
    return {'x': x, 'L0_conv_conv_w': _L0_conv_in['conv_w'], 'L0_conv_conv_b': _L0_conv_in['conv_b'], 'L0_conv_bn_g': _L0_conv_in['bn_g'], 'L0_conv_bn_b': _L0_conv_in['bn_b'], 'L0_conv_bn_m': _L0_conv_in['bn_m'], 'L0_conv_bn_v': _L0_conv_in['bn_v'], 'L0_conv_w_qkv': _L0_conv_in['w_qkv'], 'L0_conv_b_qkv': _L0_conv_in['b_qkv'], 'L0_conv_w_o': _L0_conv_in['w_o'], 'L0_conv_b_o': _L0_conv_in['b_o'], 'L0_conv_ln1_g': _L0_conv_in['ln1_g'], 'L0_conv_ln1_b': _L0_conv_in['ln1_b'], 'L0_conv_w1': _L0_conv_in['w1'], 'L0_conv_b1': _L0_conv_in['b1'], 'L0_conv_w2': _L0_conv_in['w2'], 'L0_conv_b2': _L0_conv_in['b2'], 'L0_conv_ln2_g': _L0_conv_in['ln2_g'], 'L0_conv_ln2_b': _L0_conv_in['ln2_b']}

def reference(x, L0_conv_conv_w, L0_conv_conv_b, L0_conv_bn_g, L0_conv_bn_b, L0_conv_bn_m, L0_conv_bn_v, L0_conv_w_qkv, L0_conv_b_qkv, L0_conv_w_o, L0_conv_b_o, L0_conv_ln1_g, L0_conv_ln1_b, L0_conv_w1, L0_conv_b1, L0_conv_w2, L0_conv_b2, L0_conv_ln2_g, L0_conv_ln2_b):
    import jax
    import jax.numpy as jnp

    def _L0_conv_ref(x, conv_w, conv_b, bn_g, bn_b, bn_m, bn_v, w_qkv, b_qkv, w_o, b_o, ln1_g, ln1_b, w1, b1, w2, b2, ln2_g, ln2_b):
        import jax, jax.numpy as jnp
        import numpy as np
        C = 32
        H = 110
        K = 192
        NH = 8
        EPS_BN = 1e-05
        EPS_LN = 1e-05

        def make_pos(seq_len, dim):
            pos = np.arange(seq_len, dtype=np.float32)[:, None]
            div = np.exp(np.arange(0, dim, 2, dtype=np.float32) * -(np.log(10000.0) / dim))
            pe = np.zeros((seq_len, dim), dtype=np.float32)
            pe[:, 0::2] = np.sin(pos * div)
            pe[:, 1::2] = np.cos(pos * div)
            return jnp.asarray(pe)

        def _layernorm(t, g, b):
            mu = t.mean(-1, keepdims=True)
            var = t.var(-1, keepdims=True)
            return (t - mu) / jnp.sqrt(var + EPS_LN) * g + b
        B = x.shape[0]
        y = jax.lax.conv_general_dilated(x, conv_w, window_strides=(1, 1), padding=[(15, 15), (15, 15)], rhs_dilation=(5, 5), dimension_numbers=('NCHW', 'OIHW', 'NCHW'))
        y = y + conv_b[None, :, None, None]
        scale = (bn_g / jnp.sqrt(bn_v + EPS_BN))[None, :, None, None]
        y = (y - bn_m[None, :, None, None]) * scale + bn_b[None, :, None, None]
        imp = jax.nn.sigmoid(jax.nn.gelu(y, approximate=False))
        xs = x * imp
        flat = imp[:, 0].reshape(B, -1)
        _, idx = jax.lax.top_k(flat, K)
        idx = jnp.sort(idx, axis=1)
        xf = xs.reshape(B, C, H * H).transpose(0, 2, 1)
        tokens = jnp.take_along_axis(xf, idx[:, :, None], axis=1)
        tokens = tokens + make_pos(H * H, C)[idx]
        qkv = tokens @ w_qkv.T + b_qkv
        q, k_, v = jnp.split(qkv, 3, axis=-1)
        hd = C // NH

        def heads(t):
            return t.reshape(B, K, NH, hd).transpose(0, 2, 1, 3)
        q, k_, v = (heads(q), heads(k_), heads(v))
        scores = jnp.einsum('bhqd,bhkd->bhqk', q, k_) * (1.0 / np.sqrt(hd)).astype(x.dtype)
        attn = jax.nn.softmax(scores, axis=-1)
        o = jnp.einsum('bhqk,bhkd->bhqd', attn, v).transpose(0, 2, 1, 3).reshape(B, K, C)
        o = o @ w_o.T + b_o
        t1 = _layernorm(tokens + o, ln1_g, ln1_b)
        ff = jax.nn.relu(t1 @ w1.T + b1) @ w2.T + b2
        t2 = _layernorm(t1 + ff, ln2_g, ln2_b)
        xf = xf.at[jnp.arange(B)[:, None], idx].set(t2)
        return xf.transpose(0, 2, 1).reshape(B, C, H, H)

    def _gn(v, G=32, eps=1e-05):
        B_, C_, H_, W_ = v.shape
        g = v.reshape(B_, G, C_ // G, H_, W_)
        m = jnp.mean(g, axis=(2, 3, 4), keepdims=True)
        s = jnp.var(g, axis=(2, 3, 4), keepdims=True)
        return ((g - m) / jnp.sqrt(s + eps)).reshape(v.shape)

    def _ln_c(v, eps=1e-06):
        m = jnp.mean(v, axis=1, keepdims=True)
        s = jnp.var(v, axis=1, keepdims=True)
        return (v - m) / jnp.sqrt(s + eps)

    def _ln_t(v, eps=1e-05):
        m = jnp.mean(v, axis=-1, keepdims=True)
        s = jnp.var(v, axis=-1, keepdims=True)
        return (v - m) / jnp.sqrt(s + eps)

    def _to_tokens(v):
        B_, C_, H_, W_ = v.shape
        return v.reshape(B_, C_, H_ * W_).transpose(0, 2, 1)

    def _from_tokens(t, like):
        B_, C_, H_, W_ = like.shape
        return t.transpose(0, 2, 1).reshape(B_, C_, H_, W_)
    x = x + _L0_conv_ref(_gn(x), L0_conv_conv_w, L0_conv_conv_b, L0_conv_bn_g, L0_conv_bn_b, L0_conv_bn_m, L0_conv_bn_v, L0_conv_w_qkv, L0_conv_b_qkv, L0_conv_w_o, L0_conv_b_o, L0_conv_ln1_g, L0_conv_ln1_b, L0_conv_w1, L0_conv_b1, L0_conv_w2, L0_conv_b2, L0_conv_ln2_g, L0_conv_ln2_b)
    return x

_drawn_inputs = setup_inputs


def setup_inputs(seed=0):
    import zlib

    import numpy as np

    out = dict(_drawn_inputs(seed))
    spreads = {'L0_conv_b_qkv': (0.0, 0.8),
     'L0_conv_b_o': (0.0, 2.0),
     'L0_conv_ln1_g': (1.0, 0.6),
     'L0_conv_ln1_b': (0.0, 0.8),
     'L0_conv_b1': (0.0, 2.0),
     'L0_conv_b2': (0.0, 2.0),
     'L0_conv_ln2_g': (1.0, 0.6),
     'L0_conv_ln2_b': (0.0, 0.8)}
    factors = {'L0_conv_w_qkv': 8.0, 'L0_conv_w_o': 8.0, 'L0_conv_w1': 8.0, 'L0_conv_w2': 8.0}
    for name, (base, spread) in spreads.items():
        noise = np.random.default_rng([zlib.crc32(name.encode()), seed]).standard_normal(out[name].shape)
        drawn = base * np.exp(spread * noise) if base else spread * noise
        out[name] = jnp.asarray(drawn.astype(out[name].dtype))
    for name, factor in factors.items():
        out[name] = (out[name] * factor).astype(out[name].dtype)
    return out
```

```python
import concourse.bass as bass
from concourse import mybir
from contextlib import ExitStack


def preact_conv_token_attention(
    nc, x, conv_w, conv_b, bn_g, bn_b, bn_m, bn_v, w_qkvT, b_qkv, w_oT, b_o, ln1_g, ln1_b,
    w1T, b1, w2T, b2, ln2_g, ln2_b, pos, const, out,
):
    f32, bf16, fp16, u32 = mybir.dt.float32, mybir.dt.bfloat16, mybir.dt.float16, mybir.dt.uint32
    ALU, ACT, AX = mybir.AluOpType, mybir.ActivationFunctionType, mybir.AxisListType.X

    B, C, H, _ = x.shape
    HW = H * H
    NB = 128 // C
    G = B // NB
    NH, HD = 8, C // 8
    K, HALF = 192, 96
    KS, DIL = 7, 5
    U = 28
    ROWS = [4] * 27 + [2]
    CH = U // 2
    XC, XROWS = 5, H // 5
    FCH, FL = 25, HW // 25
    EPS = 1e-5
    TOPK_STEPS = 25

    table = [nc.dram_tensor(f"table{n}", [HW * NB, C], f32).ap() for n in range(4)]
    table_jt = [t.rearrange("(j i b) c -> j i (b c)", j=H, b=NB) for t in table]
    conv_rows = nc.dram_tensor("conv_rows", [NB * KS, 7, 16, H], f32).ap()
    imp_flat = [nc.dram_tensor(f"imp_flat{n}", [NB * HW, 1], f32).ap() for n in range(2)]
    parts_dram = nc.dram_tensor("parts_dram", [G, 3, NB, H, H], bf16).ap()

    ctx = ExitStack()
    with ctx:
        def sb(name, shape, dt=f32):
            return ctx.enter_context(nc.sbuf_tensor(name, shape, dt))

        def pb(name, shape, dt=f32):
            return ctx.enter_context(nc.psum_tensor(name, shape, dt))

        counted = {}

        def raised(name, per=1, step=1):
            s = ctx.enter_context(nc.semaphore(name))
            counted[s.name] = per, step
            return s

        def upto(s, g, k=None):
            per, step = counted[s.name]
            return step * (per * g + (per if k is None else k + 1))

        NCONST = const.shape[1]
        cst = sb("cst", [128, NCONST])
        at = [0]

        def take(p, n):
            v = cst[0:p, at[0]:at[0] + n]
            at[0] += n
            return v

        ident = take(128, 128)
        ones = take(128, 128)
        tri = take(H, H)
        blk_f = take(100, 100)
        head_mask = take(128, NB * NH)
        iota_k = take(H, K)
        slot_col = take(HALF, 2)
        row_col = take(H, 1)
        first_chunk = take(100, NB)
        tab_base = take(HALF, 8)
        imp_base = take(HALF, 8)
        bones_f = take(12, 128)
        blk = sb("blk", [100, 100], fp16)
        bones = sb("bones", [12, 128], bf16)
        zrow = sb("zrow", [H, H])

        w_conv = sb("w_conv", [128, KS, 32])
        w_small = sb("w_small", [128, KS, KS])
        wq = sb("wq", [128, 128])
        wk = sb("wk", [128, 128])
        wv = sb("wv", [128, 128])
        wo = sb("wo", [128, 128])
        w1 = sb("w1", [128, 2, 128])
        w2 = sb("w2", [128, 64])
        qk_bias = sb("qk_bias", [128, 2])
        b1_col = sb("b1_col", [128, 1])
        rep = sb("rep", [HALF, 7, 2 * NB, C])
        bn = sb("bn", [H, 8])
        eps_col = sb("eps_col", [128, 2])

        X = [sb(f"X{p}", [128, H, H]) for p in range(2)]
        lent = sb("lent", [128, 2, 8, 128])
        xt = lent[0:H]
        lent_flat = lent[:].rearrange("p a r c -> p (a r c)")
        rt = sb("rt", [H, 2, 8, 128])
        imp_b = sb("imp_b", [12, 2, 8 * H], bf16)
        wgt = sb("wgt", [128, 2, 4 * H])
        res = sb("res", [128, 2, 8 * H])
        stats = sb("stats", [128, 25, 6])
        mom = sb("mom", [128, G, 6])
        cvr = sb("cvr", [128, 2, 4 * H])
        y7 = sb("y7", [H, NB, KS, H])
        yy = sb("yy", [H, NB, H])
        ge = sb("ge", [H, NB, H])
        imp = [sb(f"imp{p}", [H, NB, H]) for p in range(2)]
        flat = sb("flat", [100, FL])
        junk = sb("junk", [100, FL], bf16)
        th = sb("th", [100, 4])
        cnt = sb("cnt", [100, 1], fp16)
        tsel = sb("tsel", [100, NB])
        tb = sb("tb", [H, NB])
        gt = sb("gt", [H, NB, H], bf16)
        eq = sb("eq", [H, NB, H], bf16)
        cg = sb("cg", [H, NB, H], bf16)
        ce = sb("ce", [H, NB, H])
        tot = sb("tot", [H, 8])
        off = sb("off", [H, 16])
        startend = sb("startend", [H, 2 * NB])
        cs = sb("cs", [H, NB, 112], bf16)
        hot_a = sb("hot_a", [H, NB, K], bf16)
        hot = sb("hot", [H, NB, K], bf16)
        im = ce
        parts = sb("parts", [H, 3, NB, H], bf16)
        jcol = yy[0:HALF].rearrange("p b j -> p (b j)").bitcast(bf16).rearrange("p (k j) -> p k j", j=H)
        col = sb("col", [HALF, 8])
        pixf = sb("pixf", [HALF, 3, 8])
        idx = sb("idx", [HALF, 3, 8], u32)
        tok_x = sb("tok_x", [HALF, 8, C])
        tok_pos = sb("tok_pos", [HALF, 8, C])
        tok_imp = sb("tok_imp", [HALF, 8])
        diag = lent_flat[:, NH * K:NH * K + 256]
        tok = sb("tok", [HALF, 8, C])
        tok_t = sb("tok_t", [128, K])
        q_t = sb("q_t", [128, K])
        k_t = sb("k_t", [128, K])
        vpad = sb("vpad", [HALF, 2, NB * NH, 8])
        qm = lent_flat[:, 0:NH * K].rearrange("p (h q) -> p h q", q=K)
        pr = sb("pr", [HALF, 2, NH, K])
        mx = sb("mx", [HALF, 2, 2])
        pt = sb("pt", [HALF, 2, NH, HALF])
        o_t = sb("o_t", [128, 2, HALF])
        rden = sb("rden", [HALF, 2, 4])
        o_tok = sb("o_tok", [HALF, 2, NB, C])
        act_t = sb("act_t", [128, K])
        hid = lent_flat[:, 0:2 * K].rearrange("p (a q) -> p a q", q=K)
        ra = sb("ra", [HALF, 8, C])
        rb = sb("rb", [HALF, 8, C])
        rs = sb("rs", [HALF, 4, 8])

        cv = pb("cv", [128, 2, 512])
        tr = pb("tr", [128, 2, 512])
        ib = pb("ib", [128, 512])
        sc = pb("sc", [128, 2, 512])
        ms = pb("ms", [128, 512])

        ready = raised("ready", 1, 16)
        dve_set = raised("dve_set")
        bn_rstd = raised("bn_rstd")
        x_in = [[raised(f"x_in{p}_{c}", 1, 16) for c in range(XC)] for p in range(2)]
        xt_tr = raised("xt_tr", U)
        xt_cp = raised("xt_cp", U)
        tab_w = [raised(f"tab_w{i}", CH // 2, 16) for i in range(2)]
        var_ok = raised("var_ok")
        rstd_ok = raised("rstd_ok")
        xn_ok = raised("xn_ok", XC)
        conv_ok = raised("conv_ok", 7)
        cv_cp = raised("cv_cp", 7)
        cv_w = [raised(f"cv_w{i}", [4, 3][i], 64) for i in range(2)]
        y7_in = raised("y7_in", 1, 16 * KS)
        y_ok = raised("y_ok")
        gelu_ok = raised("gelu_ok")
        imp_ok = raised("imp_ok")
        imp_w = raised("imp_w", 1, 16)
        flat_in = raised("flat_in", 1, 16)
        cnt_ok = raised("cnt_ok", TOPK_STEPS)
        cnt_sum = raised("cnt_sum", TOPK_STEPS)
        tsel_ok = raised("tsel_ok")
        tb_ok = raised("tb_ok")
        tot_ok = raised("tot_ok")
        off_ok = raised("off_ok")
        hot_ok = raised("hot_ok")
        pick_ok = raised("pick_ok")
        im_ok = raised("im_ok")
        part_ok = raised("part_ok")
        parts_w = raised("parts_w", 1, 16)
        idx_ok = raised("idx_ok")
        tok_in = raised("tok_in", 1, 24 * 16)
        diag_ok = raised("diag_ok")
        rep_ok = raised("rep_ok")
        tok_ok = raised("tok_ok")
        tokt_ok = raised("tokt_ok")
        tokt_cp = raised("tokt_cp")
        qkv_ok = raised("qkv_ok")
        qk_cp = raised("qk_cp", 2)
        v_cp = raised("v_cp")
        qm_ok = raised("qm_ok", NB)
        s_ok = raised("s_ok", 32)
        p_sub = raised("p_sub", 32)
        p_exp = raised("p_exp", 8)
        pt_tr = raised("pt_tr", 32)
        pt_cp = raised("pt_cp", 32)
        pv_ok = raised("pv_ok", 8)
        ot_cp = raised("ot_cp", 8)
        ot_tr = raised("ot_tr", 8)
        o_ok = raised("o_ok", 8)
        oa_tr = raised("oa_tr")
        oa_cp = raised("oa_cp")
        wo_ok = raised("wo_ok")
        v1_ok = raised("v1_ok")
        r1_ok = raised("r1_ok")
        t1_ok = raised("t1_ok")
        t1_tr = raised("t1_tr")
        t1_cp = raised("t1_cp")
        h_ok = raised("h_ok")
        h_cp = raised("h_cp")
        ff_ok = raised("ff_ok")
        v2_ok = raised("v2_ok")
        r2_ok = raised("r2_ok")
        t2_ok = raised("t2_ok")
        scat = raised("scat", 1, 8 * 16)
        rt_in = [raised(f"rt_in{i}", CH // 2, 16) for i in range(2)]
        ib_in = [raised(f"ib_in{i}", CH // 2, 16 * 3) for i in range(2)]
        rt_tr = raised("rt_tr", U)
        ib_ok = raised("ib_ok", U)
        wgt_ok = raised("wgt_ok", U)
        res_ok = raised("res_ok", U)
        fin_ok = raised("fin_ok", CH)
        out_w = [raised(f"out_w{i}", CH // 2, 16) for i in range(2)]
        own = {e: ctx.enter_context(nc.semaphore(f"own_{e}")) for e in ("dve", "act", "pool")}

        block = ctx.enter_context(nc.Block())
        chunk_rows = [min(8, H - 8 * c) for c in range(CH)]
        NLOADS = 3 + 4 * 5 + 4 + 2 * 2 + 2 + 8 + 4 * 4 + 7 * 8 + 8
        loads = [0]

        def flat_unit(ap2, nr):
            return ap2[:, 0:nr * H]

        C_AFTER = {"idx": range(0, 6), "tok": range(6, 8), "post1": range(24, 26), "post2": range(26, 28)}
        C_AFTER |= {("att", n): range(8 + 2 * n, 10 + 2 * n) for n in range(8)}

        @block.sync
        def _(sp):
            def load(dst, src):
                sp.dma_start(dst, src).then_inc(ready, 16)
                loads[0] += 1

            load(cst[:], const)
            for b in range(NB):
                q = slice(C * b, C * b + C)
                load(w_small[q], conv_w)

            def load_x(g):
                if not 0 <= g < G:
                    return
                if g >= 2:
                    sp.wait_ge(conv_ok, upto(conv_ok, g - 2))
                xs = x.rearrange("(g b) c h w -> g (b c) h w", b=NB)[g]
                for c in range(XC):
                    r = slice(c * XROWS, (c + 1) * XROWS)
                    sp.dma_start(X[g % 2][:, r, :], xs[:, r, :]).then_inc(x_in[g % 2][c], 16)
            load_x(0)
            load_x(1)
            sp.wait_ge(dve_set, upto(dve_set, 0))
            for b in range(NB):
                q = slice(C * b, C * b + C)
                for n, w in enumerate((wq, wk, wv)):
                    load(w[q, q], w_qkvT[:, n * C:(n + 1) * C])
                load(wo[q, q], w_oT)
                load(w1[q, b // 2, 64 * (b % 2):64 * (b % 2) + 64], w1T)
                load(w2[64 * (b % 2):64 * (b % 2) + 64, 32 * (b % 2):32 * (b % 2) + 32], w2T) if b < 2 else None
                for n in range(2):
                    load(qk_bias[q, n:n + 1], b_qkv[n * C:(n + 1) * C].rearrange("(c o) -> c o", o=1))
            for b in range(2):
                load(b1_col[64 * b:64 * b + 64, :], b1.rearrange("(c o) -> c o", o=1))
            for n, v in enumerate((b_qkv[2 * C:3 * C], b_o, ln1_g, ln1_b, b2, ln2_g, ln2_b)):
                src = v.rearrange("(o p c) -> o p c", o=1, p=1).broadcast_to([HALF, 2 * NB, C])
                load(rep[:, n], src)
            for n, v in enumerate((conv_b, bn_g, bn_b, bn_m, bn_v)):
                load(bn[:, n:n + 1], v.rearrange("(o c) -> o c", o=1).broadcast_to([H, 1]))

            def table_out(g, c):
                if c == 0:
                    for i in range(2):
                        if g >= 4:
                            sp.wait_ge(rt_in[i], upto(rt_in[i], g - 4))
                sp.wait_ge(xt_cp, upto(xt_cp, g, 2 * c + 1))
                n = chunk_rows[c]
                sp.dma_start(table_jt[g % 4][:, 8 * c:8 * c + n, :], xt[:, c % 2, 0:n, :]).then_inc(tab_w[c % 2], 16)

            def back_in(g, c):
                if c >= CH:
                    return
                if c < 2:
                    if g >= 1:
                        sp.wait_ge(rt_tr, upto(rt_tr, g - 1))
                    if g >= 1:
                        sp.wait_ge(ib_ok, upto(ib_ok, g - 1))
                else:
                    sp.wait_ge(rt_tr, upto(rt_tr, g, 2 * (c - 2) + 1))
                    sp.wait_ge(ib_ok, upto(ib_ok, g, 2 * (c - 2) + 1))
                if c == 0:
                    sp.wait_ge(scat, upto(scat, g))
                    sp.wait_ge(parts_w, upto(parts_w, g))
                n = chunk_rows[c]
                sp.dma_start(rt[:, c % 2, 0:n, :], table_jt[g % 4][:, 8 * c:8 * c + n, :]).then_inc(rt_in[c % 2], 16)
                for part in range(3):
                    sp.dma_start(imp_b[NB * part:NB * part + NB, c % 2, 0:n * H],
                                 parts_dram[g, part, :, 8 * c:8 * c + n, :].rearrange("b i j -> b (i j)")
                                 ).then_inc(ib_in[c % 2], 16)

            def out_store(g, c):
                sp.wait_ge(fin_ok, upto(fin_ok, g, c))
                n = chunk_rows[c]
                og = out.rearrange("(g b) c h w -> g (b c) h w", b=NB)[g]
                sp.dma_start(og[:, 8 * c:8 * c + n, :].rearrange("p i j -> p (i j)"),
                                               res[:, c % 2, 0:n * H]).then_inc(out_w[c % 2], 16)

            for c in range(CH):
                table_out(0, c)
            for s in range(G + 2):
                if s + 1 < G:
                    for c in range(CH):
                        table_out(s + 1, c)
                if s + 2 < G:
                    load_x(s + 2)
                g = s - 2
                if g >= 0:
                    back_in(g, 0)
                    back_in(g, 1)
                    for c in range(CH):
                        back_in(g, c + 2)
                        out_store(g, c)
            for i in range(2):
                sp.wait_ge(out_w[i], upto(out_w[i], G - 1))

        NL = loads[0]

        def all_ready(eng):
            eng.wait_ge(ready, 16 * NL)

        @block.tensor
        def _(pe):
            mm = nc.tensor.matmul

            def unit_in(g, n):
                p, nr = g % 2, ROWS[n]
                if n == 0:
                    pe.wait_ge(x_in[p][0], upto(x_in[p][0], g // 2))
                lo, hi = 4 * n // XROWS, (4 * n + nr - 1) // XROWS
                if hi != (4 * n - 1) // XROWS and n:
                    pe.wait_ge(x_in[p][hi], upto(x_in[p][hi], g // 2))
                if n >= 2:
                    pe.wait_ge(xt_cp, upto(xt_cp, g, n - 2))
                else:
                    if g >= 1:
                        pe.wait_ge(xt_cp, upto(xt_cp, g - 1, U - 2 + n))
                    if g >= 4:
                        pe.wait_ge(res_ok, upto(res_ok, g - 4, U - 2 + n))
                    if g >= 4:
                        pe.wait_ge(wgt_ok, upto(wgt_ok, g - 4, U - 2 + n))
                for r in range(nr):
                    last = nc.tensor.transpose(tr[0:H, n % 2, 128 * r:128 * r + 128], X[p][:, 4 * n + r, :], ident)
                last.then_inc(xt_tr, 1)

            def conv_part(g, t, part):
                p = g % 2
                order = [3, 0, 1, 2, 4, 5, 6]
                for n in range(7 * part, 7 * part + 7):
                    kj, q = order[n // 4], n % 4
                    u = 4 * t + q
                    s, nr = DIL * (kj - 3), ROWS[u]
                    j0, j1 = max(0, -s), min(H, H - s)
                    o = cv[32 * q:32 * q + 32, t % 2, 0:nr * H].rearrange("p (r j) -> p r j", j=H)
                    last = mm(o[:, :, j0:j1], w_conv[:, kj, :], X[p][:, 4 * u:4 * u + nr, j0 + s:j1 + s],
                              start=n < 4, stop=n >= 24, skip_group_check=True)
                if part == 3:
                    last.then_inc(conv_ok, 1)

            def count(g, n):
                pe.wait_ge(cnt_ok, upto(cnt_ok, g, n))
                mm(ms[0:100, n:n + 1], blk[:], cnt[:], start=True, stop=True).then_inc(cnt_sum, 1)

            def unit_back(g, n):
                c, k, nr = n // 2, n % 2, ROWS[n]
                if k == 0:
                    pe.wait_ge(rt_in[c % 2], upto(rt_in[c % 2], g, c // 2))
                    pe.wait_ge(ib_in[c % 2], upto(ib_in[c % 2], g, c // 2))
                if n >= 2:
                    pe.wait_ge(res_ok, upto(res_ok, g, n - 2))
                else:
                    pe.wait_ge(xt_cp, upto(xt_cp, min(g + 3, G - 1), U - 2 + n))
                    if g > 0:
                        if g >= 1:
                            pe.wait_ge(res_ok, upto(res_ok, g - 1, U - 2 + n))
                for r in range(nr):
                    last = nc.tensor.transpose(tr[:, n % 2, H * r:H * r + H], rt[:, c % 2, 4 * k + r, :], ident[0:H, 0:H])
                last.then_inc(rt_tr, 1)
                if n:
                    pe.wait_ge(wgt_ok, upto(wgt_ok, g, n - 1))
                else:
                    if g >= 1:
                        pe.wait_ge(wgt_ok, upto(wgt_ok, g - 1))
                mm(ib[:, 0:nr * H], bones[:], imp_b[:, c % 2, 4 * k * H:(4 * k + nr) * H], start=True, stop=True).then_inc(ib_ok, 1)

            def back(g, key):
                if g >= 0:
                    for n in C_AFTER[key]:
                        unit_back(g, n)

            def find(g):
                pe.wait_ge(tsel_ok, upto(tsel_ok, g))
                mm(ms[0:H, 32:32 + NB], ones[0:100, 0:H], tsel[:], start=True, stop=True).then_inc(tb_ok, 1)
                pe.wait_ge(tot_ok, upto(tot_ok, g))
                mm(ms[0:H, 40:48], tri, tot[:], start=True, stop=True)
                mm(ms[0:H, 48:56], ones[0:H, 0:H], tot[:], start=True, stop=True).then_inc(off_ok, 1)
                pe.wait_ge(hot_ok, upto(hot_ok, g))
                for half in range(2):
                    for b in range(NB):
                        last = mm(sc[0:HALF, half, 112 * b:112 * b + 111], hot[:, b, HALF * half:HALF * half + HALF],
                                  cs[:, b, 0:111], start=True, stop=True)
                last.then_inc(pick_ok, 1)
                pe.wait_ge(diag_ok, upto(diag_ok, g))
                pe.wait_ge(cv_cp, upto(cv_cp, min(g + 1, G - 1)))
                mm(cv[0:HALF, 0, 0:256], ones[:, 0:HALF], diag, start=True, stop=True).then_inc(rep_ok, 1)

            def two_transposes(flag, src, bank):
                for half in range(2):
                    last = nc.tensor.transpose(cv[:, bank, HALF * half:HALF * half + HALF], src(half), ident[0:HALF, 0:HALF])
                last.then_inc(flag, 1)

            def embed(g):
                pe.wait_ge(tok_ok, upto(tok_ok, g))
                two_transposes(tokt_ok, lambda h: tok[:, NB * h:NB * h + NB, :].rearrange("p b c -> p (b c)"), 1)
                pe.wait_ge(tokt_cp, upto(tokt_cp, g))
                mm(sc[:, 0, 0:K], wq[:], tok_t[:], start=True, stop=True)
                mm(sc[:, 1, 0:K], wk[:], tok_t[:], start=True, stop=True)
                for half in range(2):
                    last = mm(ms[0:HALF, 128 * half:128 * half + 128], tok_t[:, HALF * half:HALF * half + HALF], wv[:],
                              start=True, stop=True)
                last.then_inc(qkv_ok, 1)
                pe.wait_ge(qk_cp, upto(qk_cp, g))

            def scores(g, n):
                b, half = n // 2, n % 2
                if half == 0:
                    pe.wait_ge(qm_ok, upto(qm_ok, g, b))
                for pair in range(4):
                    k = 4 * n + pair
                    if k >= 2:
                        pe.wait_ge(p_sub, upto(p_sub, g, k - 2))
                    for h in range(2):
                        last = mm(sc[0:HALF, k % 2, K * h:K * h + K], qm[:, 2 * pair + h, HALF * half:HALF * half + HALF],
                                  k_t[:], start=True, stop=True)
                    last.then_inc(s_ok, 1)

            def attend(g, n):
                b, half = n // 2, n % 2
                pe.wait_ge(p_exp, upto(p_exp, g, n))
                for kh in range(2):
                    for hg in range(2):
                        k = 4 * n + 2 * kh + hg
                        if k >= 2:
                            pe.wait_ge(pt_cp, upto(pt_cp, g, k - 2))
                        for h in range(4):
                            last = nc.tensor.transpose(cv[0:HALF, hg, HALF * h:HALF * h + HALF],
                                                       pr[:, n % 2, 4 * hg + h, HALF * kh:HALF * kh + HALF], ident[0:HALF, 0:HALF])
                        last.then_inc(pt_tr, 1)
                if n == 0:
                    pe.wait_ge(v_cp, upto(v_cp, g))
                pe.wait_ge(pt_cp, upto(pt_cp, g, 4 * n + 3))
                if n:
                    pe.wait_ge(o_ok, upto(o_ok, g, n - 1))
                for hh in range(2):
                    for kh in range(2):
                        for q in range(4):
                            h = 4 * hh + q
                            last = mm(ms[32 * q:32 * q + 8, HALF * hh:HALF * hh + HALF], vpad[:, kh, NH * b + h, :],
                                      pt[:, kh, h, :], start=kh == 0, stop=kh == 1, skip_group_check=True)
                last.then_inc(pv_ok, 1)
                pe.wait_ge(ot_cp, upto(ot_cp, g, n))
                for hh in range(2):
                    last = nc.tensor.transpose(ms[0:HALF, 256 + 128 * hh:384 + 128 * hh], o_t[:, hh, :], ident)
                last.then_inc(ot_tr, 1)

            def mix(g):
                pe.wait_ge(o_ok, upto(o_ok, g))
                two_transposes(oa_tr, lambda h: o_tok[:, h].rearrange("p b c -> p (b c)"), 0)
                pe.wait_ge(oa_cp, upto(oa_cp, g))
                for half in range(2):
                    last = mm(ms[0:HALF, 128 * half:128 * half + 128], act_t[:, HALF * half:HALF * half + HALF], wo[:],
                              start=True, stop=True)
                last.then_inc(wo_ok, 1)

            def feed(g):
                pe.wait_ge(t1_ok, upto(t1_ok, g))
                two_transposes(t1_tr, lambda h: ra[:, NB * h:NB * h + NB, :].rearrange("p b c -> p (b c)"), 1)
                pe.wait_ge(t1_cp, upto(t1_cp, g))
                for pair in range(2):
                    last = mm(cv[:, 0, K * pair:K * pair + K], w1[:, pair, :], act_t[:], start=True, stop=True)
                last.then_inc(h_ok, 1)
                pe.wait_ge(h_cp, upto(h_cp, g))
                for half in range(2):
                    for pair in range(2):
                        last = mm(ms[0:HALF, 128 * half + 64 * pair:128 * half + 64 * pair + 64],
                                  hid[:, pair, HALF * half:HALF * half + HALF], w2[:], start=True, stop=True)
                last.then_inc(ff_ok, 1)

            all_ready(pe)
            pe.wait_ge(dve_set, upto(dve_set, 0))
            pe.wait_ge(dve_set, 2)
            for n in range(U):
                unit_in(0, n)
            for s in range(G + 2):
                now, topk, ahead, end = s, s - 1, s + 1, s - 2
                if now < G:
                    pe.wait_ge(xn_ok, upto(xn_ok, now))
                for t in range(7):
                    if now < G:
                        if t >= 2:
                            pe.wait_ge(cv_cp, upto(cv_cp, now, t - 2))
                        else:
                            if now >= 1:
                                pe.wait_ge(cv_cp, upto(cv_cp, now - 1))
                        if t == 0 and now:
                            if now >= 2:
                                pe.wait_ge(h_cp, upto(h_cp, now - 2))
                            if now >= 2:
                                pe.wait_ge(t1_cp, upto(t1_cp, now - 2))
                            if now >= 2:
                                pe.wait_ge(pt_cp, upto(pt_cp, now - 2))
                            if now >= 2:
                                pe.wait_ge(tokt_cp, upto(tokt_cp, now - 2))
                    for part in range(4):
                        n = 4 * t + part
                        if now < G:
                            conv_part(now, t, part)
                        if 0 <= topk < G and n < TOPK_STEPS:
                            count(topk, n)
                        if ahead < G:
                            unit_in(ahead, n)
                if 0 <= topk < G:
                    find(topk)
                back(end, "idx")
                if 0 <= topk < G:
                    embed(topk)
                back(end, "tok")
                if 0 <= topk < G:
                    scores(topk, 0)
                for n in range(8):
                    if 0 <= topk < G:
                        if n < 7:
                            scores(topk, n + 1)
                        attend(topk, n)
                    back(end, ("att", n))
                if 0 <= topk < G:
                    mix(topk)
                back(end, "post1")
                if 0 <= topk < G:
                    feed(topk)
                back(end, "post2")

        @block.scalar
        def _(act):
            mine = [0]

            def link(ins):
                mine[0] += 1
                ins.then_inc(own["act"], 1)
                act.wait_ge(own["act"], mine[0])

            A = nc.scalar.activation

            def unit_in(g, n):
                nr, c = ROWS[n], n // 2
                act.wait_ge(xt_tr, upto(xt_tr, g, n))
                if n == 0:
                    if g >= 3:
                        act.wait_ge(ff_ok, upto(ff_ok, g - 3))
                if n % 2 == 0:
                    if c >= 2:
                        act.wait_ge(tab_w[c % 2], upto(tab_w[c % 2], g, c // 2 - 1))
                    else:
                        if g >= 1:
                            act.wait_ge(tab_w[c % 2], upto(tab_w[c % 2], g - 1))
                k = 4 * (n % 2)
                nc.scalar.copy(xt[:, c % 2, k:k + nr, :].rearrange("p r c -> p (r c)"),
                                          tr[0:H, n % 2, 0:128 * nr]).then_inc(xt_cp, 1)

            def round_copy(g, t):
                act.wait_ge(conv_ok, upto(conv_ok, g, t))
                if t >= 2:
                    act.wait_ge(cv_w[t % 2], upto(cv_w[t % 2], g, t // 2 - 1))
                else:
                    if g >= 1:
                        act.wait_ge(cv_w[t % 2], upto(cv_w[t % 2], g - 1))
                if t < 6:
                    nc.scalar.copy(cvr[:, t % 2, :], cv[:, t % 2, 0:4 * H]).then_inc(cv_cp, 1)
                else:
                    link(nc.scalar.copy(cvr[96:128, 0, 0:2 * H], cv[96:128, 0, 0:2 * H]))
                    nc.scalar.copy(cvr[0:96, 0, :], cv[0:96, 0, 0:4 * H]).then_inc(cv_cp, 1)

            def round_out(g, t):
                act.wait_ge(cv_cp, upto(cv_cp, g, t))
                if t == 0:
                    if g >= 1:
                        act.wait_ge(y7_in, upto(y7_in, g - 1))
                for q in range(4):
                    act.dma_start(conv_rows[:, t, 4 * q:4 * q + 4, :].rearrange("p r j -> p (r j)"),
                                  cvr[32 * q:32 * q + NB * KS, t % 2, :]).then_inc(cv_w[t % 2], 16)

            def taps_in(g):
                for i in range(2):
                    act.wait_ge(cv_w[i], upto(cv_w[i], g))
                if g >= 1:
                    act.wait_ge(y_ok, upto(y_ok, g - 1))
                rows = conv_rows.rearrange("(b k) t r j -> k (t r) b j", k=KS)
                for ki in range(KS):
                    o = DIL * (ki - 3)
                    i0, i1 = max(0, -o), min(H, H - o)
                    act.dma_start(y7[i0:i1, :, ki, :], rows[ki, i0 + o:i1 + o, :, :]).then_inc(y7_in, 16)

            def importance(g):
                act.wait_ge(y_ok, upto(y_ok, g))
                link(A(ge[:].rearrange("p b j -> p (b j)"), yy[:].rearrange("p b j -> p (b j)"), ACT.Gelu,
                       scale=bn[:, 5:6], bias=bn[:, 6:7]))
                A(ge[:], ge[:], ACT.Exp, scale=-1.0).then_inc(gelu_ok, 1)

            def imp_out(g):
                act.wait_ge(imp_ok, upto(imp_ok, g))
                if g >= 2:
                    act.wait_ge(tok_in, upto(tok_in, g - 2))
                act.dma_start(imp_flat[g % 2].rearrange("(b i j) o -> i b (j o)", b=NB, i=H), imp[g % 2][:]).then_inc(imp_w, 16)

            def flat_load(g):
                act.wait_ge(imp_w, upto(imp_w, g))
                if g >= 1:
                    act.wait_ge(cnt_ok, upto(cnt_ok, g - 1))
                act.dma_start(flat[:], imp_flat[g % 2].rearrange("(p f) o -> p (f o)", f=FL)).then_inc(flat_in, 16)

            def unit_back(g, n):
                nr = ROWS[n]
                act.wait_ge(ib_ok, upto(ib_ok, g, n))
                if n >= 2:
                    act.wait_ge(res_ok, upto(res_ok, g, n - 2))
                else:
                    if g >= 1:
                        act.wait_ge(res_ok, upto(res_ok, g - 1, U - 2 + n))
                A(wgt[:, n % 2, 0:nr * H], ib[:, 0:nr * H], ACT.Identity, scale=mom[:, g, 2:3], bias=eps_col[:, 1:2]).then_inc(wgt_ok, 1)

            def back(g, key):
                if g >= 0:
                    for n in C_AFTER[key]:
                        unit_back(g, n)

            def parts_out(g):
                act.wait_ge(part_ok, upto(part_ok, g))
                act.dma_start(parts_dram[g].rearrange("q b i j -> i (q b) j"),
                                           parts[:].rearrange("p q b j -> p (q b) j")).then_inc(parts_w, 16)

            def embed(g):
                act.wait_ge(tokt_ok, upto(tokt_ok, g))
                nc.scalar.copy(tok_t[:], cv[:, 1, 0:K]).then_inc(tokt_cp, 1)
                act.wait_ge(qkv_ok, upto(qkv_ok, g))
                A(q_t[:], sc[:, 0, 0:K], ACT.Identity, scale=HD ** -0.5, bias=qk_bias[:, 0:1]).then_inc(qk_cp, 1)
                A(k_t[:], sc[:, 1, 0:K], ACT.Identity, bias=qk_bias[:, 1:2]).then_inc(qk_cp, 1)

            def exps(g, n):
                act.wait_ge(p_sub, upto(p_sub, g, 4 * n + 3))
                A(pr[:, n % 2], pr[:, n % 2], ACT.Exp).then_inc(p_exp, 1)

            def attend(g, n):
                for k in range(4 * n, 4 * n + 4):
                    act.wait_ge(pt_tr, upto(pt_tr, g, k))
                    if k % 4 == 0 and n:
                        act.wait_ge(pv_ok, upto(pv_ok, g, n - 1))
                    kh, hg = (k // 2) % 2, k % 2
                    nc.scalar.copy(pt[:, kh, 4 * hg:4 * hg + 4, :], cv[0:HALF, hg, 0:4 * HALF].rearrange("p (h q) -> p h q", q=HALF)).then_inc(pt_cp, 1)
                act.wait_ge(pv_ok, upto(pv_ok, g, n))
                if n:
                    act.wait_ge(ot_tr, upto(ot_tr, g, n - 1))
                else:
                    if g >= 1:
                        act.wait_ge(ot_tr, upto(ot_tr, g - 1))
                nc.scalar.copy(o_t[:], ms[:, 0:2 * HALF].rearrange("p (a q) -> p a q", a=2)).then_inc(ot_cp, 1)

            def mix(g):
                act.wait_ge(oa_tr, upto(oa_tr, g))
                nc.scalar.copy(act_t[:], cv[:, 0, 0:K]).then_inc(oa_cp, 1)

            def feed(g):
                act.wait_ge(t1_tr, upto(t1_tr, g))
                nc.scalar.copy(act_t[:], cv[:, 1, 0:K]).then_inc(t1_cp, 1)
                act.wait_ge(h_ok, upto(h_ok, g))
                A(hid.rearrange("p a q -> p (a q)"), cv[:, 0, 0:2 * K], ACT.Relu, bias=b1_col[:]).then_inc(h_cp, 1)

            all_ready(act)
            act.wait_ge(dve_set, 2)
            link(nc.scalar.mul(qk_bias[:, 0:1], qk_bias[:, 0:1], HD ** -0.5))
            for n in range(U):
                unit_in(0, n)
            for s in range(G + 2):
                now, topk, ahead, end = s, s - 1, s + 1, s - 2
                for t in range(7):
                    for part in range(4):
                        if ahead < G:
                            unit_in(ahead, 4 * t + part)
                        if now < G and part == 1 and t:
                            round_out(now, t - 1)
                    if now < G:
                        round_copy(now, t)
                if now < G:
                    round_out(now, 6)
                if 0 <= topk < G:
                    parts_out(topk)
                if now < G:
                    taps_in(now)
                back(end, "idx")
                if now < G:
                    importance(now)
                if 0 <= topk < G:
                    embed(topk)
                back(end, "tok")
                if now < G:
                    imp_out(now)
                if 0 <= topk < G:
                    exps(topk, 0)
                for n in range(8):
                    if 0 <= topk < G:
                        if n < 7:
                            exps(topk, n + 1)
                        attend(topk, n)
                    if now < G and n == 1:
                        flat_load(now)
                    back(end, ("att", n))
                if 0 <= topk < G:
                    mix(topk)
                back(end, "post1")
                if 0 <= topk < G:
                    feed(topk)
                back(end, "post2")

        @block.gpsimd
        def _(pool):
            gp = nc.gpsimd
            mine = [0]

            def link(ins):
                mine[0] += 1
                ins.then_inc(own["pool"], 1)
                pool.wait_ge(own["pool"], mine[0])

            def normalise(g):
                pool.wait_ge(var_ok, upto(var_ok, g))
                gp.tensor_tensor(mom[:, g, 2:3], mom[:, g, 4:5], eps_col[:, 0:1], ALU.pow).then_inc(rstd_ok, 1)
                pool.wait_ge(rstd_ok, upto(rstd_ok, g))
                pool.wait_ge(xt_tr, upto(xt_tr, g))
                for c in range(XC):
                    v = X[g % 2][:, c * XROWS:(c + 1) * XROWS, :].rearrange("p r j -> p (r j)")
                    gp.tensor_scalar(v, v, mom[:, g, 3:4], mom[:, g, 2:3], ALU.add, ALU.mult).then_inc(xn_ok, 1)

            def split(g):
                pool.wait_ge(im_ok, upto(im_ok, g))
                if g >= 1:
                    pool.wait_ge(parts_w, upto(parts_w, g - 1))
                for n in range(3):
                    if n < 2:
                        link(gp.tensor_copy(parts[:, n], im[:]))
                        link(gp.tensor_tensor(im[:], im[:], parts[:, n], ALU.subtract))
                    else:
                        gp.tensor_copy(parts[:, n], im[:]).then_inc(part_ok, 1)

            def gather(g):
                pool.wait_ge(idx_ok, upto(idx_ok, g))
                for i in range(2):
                    pool.wait_ge(tab_w[i], upto(tab_w[i], g))
                pool.wait_ge(imp_w, upto(imp_w, g))
                if g:
                    if g >= 1:
                        pool.wait_ge(scat, upto(scat, g - 1))
                for k in range(8):
                    for dst, src, n in ((tok_x[:, k, :], table[g % 4], 0), (tok_imp[:, k:k + 1], imp_flat[g % 2], 1), (tok_pos[:, k, :], pos, 2)):
                        gp.indirect_dma_start(dst, None, src, bass.IndirectOffsetOnAxis(ap=idx[:, n, k:k + 1], axis=0)
                                              ).then_inc(tok_in, 16)

            def masked(g, b):
                if b == 0:
                    pool.wait_ge(qk_cp, upto(qk_cp, g, 0))
                    for i in range(2):
                        pool.wait_ge(tab_w[i], upto(tab_w[i], min(g + 2, G - 1)))
                else:
                    pool.wait_ge(s_ok, upto(s_ok, g, 8 * b - 1))
                for h in range(NH):
                    last = gp.tensor_scalar(qm[:, h, :], q_t[:], head_mask[:, NH * b + h:NH * b + h + 1], 1.0, ALU.mult, ALU.mult)
                last.then_inc(qm_ok, 1)

            def power(g, src, dst, done):
                pool.wait_ge(src, upto(src, g))
                gp.tensor_tensor(dst, rs[:, 1, :], eps_col[0:HALF, 0:1].broadcast_to([HALF, 8]), ALU.pow).then_inc(done, 1)

            def scatter(g):
                pool.wait_ge(t2_ok, upto(t2_ok, g))
                for k in range(8):
                    gp.indirect_dma_start(table[g % 4], bass.IndirectOffsetOnAxis(ap=idx[:, 0, k:k + 1], axis=0), rb[:, k, :], None
                                          ).then_inc(scat, 16)

            def finish(g, key):
                if g < 0:
                    return
                for n in C_AFTER[key]:
                    if n % 2:
                        c = n // 2
                        pool.wait_ge(res_ok, upto(res_ok, g, n))
                        v = res[:, c % 2, 0:chunk_rows[c] * H]
                        gp.tensor_scalar(v, v, 1.0, mom[:, g, 0:1], ALU.mult, ALU.add).then_inc(fin_ok, 1)

            all_ready(pool)
            pool.wait_ge(dve_set, 2)
            gp.tensor_tensor(bn[:, 7:8], bn[:, 7:8], eps_col[0:H, 0:1], ALU.pow).then_inc(bn_rstd, 1)
            normalise(0)
            for s in range(G + 2):
                now, topk, ahead, end = s, s - 1, s + 1, s - 2
                if 0 <= topk < G:
                    gather(topk)
                    split(topk)
                if ahead < G:
                    normalise(ahead)
                finish(end, "idx")
                if 0 <= topk < G:
                    masked(topk, 0)
                finish(end, "tok")
                for n in range(8):
                    if 0 <= topk < G and n % 2 == 1 and n < 7:
                        masked(topk, (n + 1) // 2)
                    finish(end, ("att", n))
                if 0 <= topk < G:
                    power(topk, v1_ok, rs[:, 2, :], r1_ok)
                finish(end, "post1")
                if 0 <= topk < G:
                    power(topk, v2_ok, rs[:, 2, :], r2_ok)
                finish(end, "post2")
                if 0 <= topk < G:
                    scatter(topk)

        @block.vector
        def _(dve):
            v = nc.vector
            mine = [0]

            def post(ins):
                mine[0] += 1
                ins.then_inc(own["dve"], 1)

            def sync():
                dve.wait_ge(own["dve"], mine[0])

            def link(ins):
                post(ins)
                sync()

            def piece(g, n):
                if n % 5 == 0:
                    dve.wait_ge(x_in[g % 2][n // 5], upto(x_in[g % 2][n // 5], g // 2))
                post(v.bn_stats(stats[:, n, :], X[g % 2][:].rearrange("p i j -> p (i j)")[:, n * FL:(n + 1) * FL]))

            def moments(g):
                sync()
                link(v.bn_aggr(mom[:, g, 0:2], stats[:].rearrange("p a b -> p (a b)")))
                link(v.tensor_scalar(mom[:, g, 3:4], mom[:, g, 0:1], -1.0, None, ALU.mult))
                v.tensor_scalar(mom[:, g, 4:5], mom[:, g, 1:2], EPS, None, ALU.add).then_inc(var_ok, 1)

            def topk_first(g):
                dve.wait_ge(flat_in, upto(flat_in, g))
                link(v.memset(th[:, 0:1], 0.4375 + 0.5))
                count(g, 0)

            def count(g, n):
                if n:
                    dve.wait_ge(cnt_sum, upto(cnt_sum, g, n - 1))
                v.tensor_scalar(junk[:], flat[:], th[:, 0:1], None, ALU.is_ge, ALU.add, accum_out=cnt[:]).then_inc(cnt_ok, 1)

            def refine(g, n):
                dve.wait_ge(cnt_sum, upto(cnt_sum, g, n))
                step = 2.0 ** -(n + 1)
                if n < TOPK_STEPS - 2:
                    link(v.tensor_scalar(th[:, 1:2], ms[0:100, n:n + 1], K - 0.5, step, ALU.is_ge, ALU.mult))
                    link(v.scalar_tensor_tensor(th[:, 0:1], th[:, 1:2], -step / 2, th[:, 0:1], op0=ALU.add, op1=ALU.add))
                elif n == TOPK_STEPS - 2:
                    link(v.tensor_scalar(th[:, 1:2], ms[0:100, n:n + 1], K - 0.5, step, ALU.is_ge, ALU.mult))
                    link(v.scalar_tensor_tensor(th[:, 2:3], th[:, 1:2], -step, th[:, 0:1], op0=ALU.add, op1=ALU.add))
                    link(v.tensor_scalar(th[:, 0:1], th[:, 2:3], step / 2, None, ALU.add))
                else:
                    link(v.tensor_scalar(th[:, 1:2], ms[0:100, n:n + 1], K - 0.5, step, ALU.is_ge, ALU.mult))
                    link(v.tensor_tensor(th[:, 3:4], th[:, 1:2], th[:, 2:3], ALU.add))

            def find(g):
                im_g = imp[g % 2]
                v.tensor_scalar(tsel[:], first_chunk, th[:, 3:4], None, ALU.mult).then_inc(tsel_ok, 1)
                dve.wait_ge(tb_ok, upto(tb_ok, g))
                link(v.tensor_copy(tb[:], ms[0:H, 32:32 + NB]))
                for b in range(NB):
                    post(v.tensor_scalar(gt[:, b], im_g[:, b], tb[:, b:b + 1], None, ALU.is_gt))
                    post(v.tensor_scalar(eq[:, b], im_g[:, b], tb[:, b:b + 1], None, ALU.is_equal))
                sync()
                for b in range(NB):
                    post(v.tensor_tensor_scan(cg[:, b], gt[:, b], zrow[:], 0.0, ALU.add, ALU.add))
                    post(v.tensor_tensor_scan(ce[:, b], eq[:, b], zrow[:], 0.0, ALU.add, ALU.add))
                sync()
                link(v.tensor_copy(tot[:, 0:NB], cg[:, :, H - 1]))
                v.tensor_copy(tot[:, NB:2 * NB], ce[:, :, H - 1]).then_inc(tot_ok, 1)
                dve.wait_ge(off_ok, upto(off_ok, g))
                post(v.tensor_copy(off[:, 0:8], ms[0:H, 40:48]))
                link(v.tensor_scalar(off[:, 8:12], ms[0:H, 48:52], -1.0, float(K), ALU.mult, ALU.add))
                for b in range(NB):
                    post(v.tensor_scalar(ce[:, b], ce[:, b], off[:, 4 + b:5 + b], off[:, 8 + b:9 + b], ALU.add, ALU.min))
                post(v.tensor_tensor(off[:, 12:16], off[:, 4:8], off[:, 8:12], ALU.min))
                sync()
                for b in range(NB):
                    post(v.scalar_tensor_tensor(cs[:, b, 0:H], cg[:, b], off[:, b:b + 1], ce[:, b], op0=ALU.add, op1=ALU.add))
                link(v.tensor_tensor(startend[:, 0:NB], off[:, 0:4], off[:, 12:16], ALU.add))
                link(v.tensor_copy(startend[:, NB:2 * NB], cs[:, :, H - 1]))
                for b in range(NB):
                    post(v.tensor_scalar(hot_a[:, b], iota_k, startend[:, b:b + 1], None, ALU.is_ge))
                sync()
                for b in range(NB):
                    last = v.scalar_tensor_tensor(hot[:, b], iota_k, startend[:, NB + b:NB + b + 1], hot_a[:, b],
                                                  op0=ALU.is_lt, op1=ALU.mult)
                    if b < NB - 1:
                        link(last)
                last.then_inc(hot_ok, 1)
                post(v.tensor_tensor(gt[:, :, 1:H], cs[:, :, 1:H], cs[:, :, 0:H - 1], ALU.subtract))
                post(v.tensor_tensor(gt[:, :, 0], cs[:, :, 0], startend[:, 0:NB], ALU.subtract))
                sync()
                if g >= 1:
                    dve.wait_ge(part_ok, upto(part_ok, g - 1))
                v.scalar_tensor_tensor(im[:].rearrange("p b j -> p (b j)"), gt[:].rearrange("p b j -> p (b j)"), 0.5,
                                                  im_g[:].rearrange("p b j -> p (b j)"), op0=ALU.is_lt, op1=ALU.mult).then_inc(im_ok, 1)
                dve.wait_ge(pick_ok, upto(pick_ok, g))
                for half in range(2):
                    for b in range(NB):
                        k = NB * half + b
                        post(v.tensor_scalar(jcol[:, k], sc[0:HALF, half, 112 * b:112 * b + H], slot_col[:, half:half + 1], None,
                                             ALU.is_le, ALU.add, accum_out=col[:, k:k + 1]))
                sync()
                if g >= 1:
                    dve.wait_ge(scat, upto(scat, g - 1))
                for half in range(2):
                    ks = slice(NB * half, NB * half + NB)
                    rows = sc[0:HALF, half, 0:448].rearrange("p (b j) -> p b j", j=112)[:, :, 110]
                    post(v.scalar_tensor_tensor(pixf[:, 2, ks], rows, float(H), col[:, ks], op0=ALU.mult, op1=ALU.add))
                    post(v.scalar_tensor_tensor(pixf[:, 0, ks], col[:, ks], float(H), rows, op0=ALU.mult, op1=ALU.add))
                sync()
                post(v.scalar_tensor_tensor(pixf[:, 0], pixf[:, 0], float(NB), tab_base, op0=ALU.mult, op1=ALU.add))
                post(v.tensor_tensor(pixf[:, 1], pixf[:, 2], imp_base, ALU.add))
                sync()
                v.tensor_copy(idx[:], pixf[:]).then_inc(idx_ok, 1)
                for i in range(2):
                    dve.wait_ge(tab_w[i], upto(tab_w[i], min(g + 2, G - 1)))
                post(v.tensor_scalar(diag[:, 0:128], ident, mom[:, g, 0:1], None, ALU.mult))
                sync()
                v.tensor_scalar(diag[:, 128:256], ident, mom[:, g, 2:3], None, ALU.mult).then_inc(diag_ok, 1)

            def importance_sum(g):
                dve.wait_ge(y7_in, upto(y7_in, g))
                v.reduce_sum(yy[:], y7[:].rearrange("p b k j -> p b j k"), AX).then_inc(y_ok, 1)

            def importance(g):
                dve.wait_ge(gelu_ok, upto(gelu_ok, g))
                link(v.tensor_scalar(yy[:], ge[:], 1.0, None, ALU.add))
                v.reciprocal(imp[g % 2][:], yy[:]).then_inc(imp_ok, 1)

            def embed(g):
                dve.wait_ge(tok_in, upto(tok_in, g))
                dve.wait_ge(rep_ok, upto(rep_ok, g))
                m = cv[0:HALF, 0, 0:128].rearrange("p (b c) -> p b c", c=C)
                r = cv[0:HALF, 0, 128:256].rearrange("p (b c) -> p b c", c=C)
                for half in range(2):
                    ks = slice(NB * half, NB * half + NB)
                    post(v.tensor_tensor(tok[:, ks], tok_x[:, ks], m, ALU.subtract))
                sync()
                for half in range(2):
                    ks = slice(NB * half, NB * half + NB)
                    post(v.tensor_tensor(tok[:, ks], tok[:, ks], r, ALU.mult))
                sync()
                link(v.tensor_tensor(tok[:], tok[:], tok_imp[:].unsqueeze(2).to_broadcast([HALF, 8, C]), ALU.mult))
                v.tensor_tensor(tok[:], tok[:], tok_pos[:], ALU.add).then_inc(tok_ok, 1)
                dve.wait_ge(qkv_ok, upto(qkv_ok, g))
                for half in range(2):
                    last = v.tensor_tensor(vpad[:, half, :, 0:HD],
                                           ms[0:HALF, 128 * half:128 * half + 128].rearrange("p (h d) -> p h d", d=HD),
                                           rep[:, 0, 0:NB].rearrange("p b (h d) -> p (b h) d", d=HD), ALU.add)
                    if half == 0:
                        link(last)
                last.then_inc(v_cp, 1)

            def soft(g, n):
                if n >= 2:
                    dve.wait_ge(pt_tr, upto(pt_tr, g, 4 * (n - 2) + 3))
                for pair in range(4):
                    k = 4 * n + pair
                    dve.wait_ge(s_ok, upto(s_ok, g, k))
                    s = sc[0:HALF, k % 2, 0:2 * K].rearrange("p (h q) -> p h q", q=K)
                    link(v.reduce_max(mx[:, k % 2], s, AX))
                    v.tensor_tensor(pr[:, n % 2, 2 * pair:2 * pair + 2], s,
                                               mx[:, k % 2].unsqueeze(2).to_broadcast([HALF, 2, K]), ALU.subtract).then_inc(p_sub, 1)

            def attend(g, n):
                b, half = n // 2, n % 2
                dve.wait_ge(ot_tr, upto(ot_tr, g, n))
                o = ms[0:HALF, 256:512].rearrange("p (h d) -> p h d", d=32)
                link(v.reciprocal(rden[:].rearrange("p a h -> p (a h)"), o[:, :, HD]))
                v.tensor_tensor(o_tok[:, half, b].rearrange("p (h d) -> p h d", d=HD), o[:, :, 0:HD],
                                          rden[:].rearrange("p a h -> p (a h)").unsqueeze(2).to_broadcast([HALF, NH, HD]), ALU.mult).then_inc(o_ok, 1)

            def norm_first(src_flag, g, add, res_in, out_v, flag):
                dve.wait_ge(src_flag, upto(src_flag, g))
                y = ms[0:HALF, 0:256].rearrange("p (k c) -> p k c", c=C)
                link(v.tensor_tensor(out_v[:], y, rep[:, add], ALU.add))
                link(v.tensor_tensor(out_v[:], out_v[:], res_in[:], ALU.add))
                link(v.reduce_sum(rs[:, 0, :], out_v[:], AX))
                link(v.tensor_scalar(rs[:, 0, :], rs[:, 0, :], 1.0 / C, None, ALU.mult))
                link(v.tensor_tensor(out_v[:], out_v[:], rs[:, 0, :].unsqueeze(2).to_broadcast([HALF, 8, C]), ALU.subtract))
                link(v.tensor_tensor(tok_pos[:], out_v[:], out_v[:], ALU.mult))
                link(v.reduce_sum(rs[:, 3, :], tok_pos[:], AX))
                v.tensor_scalar(rs[:, 1, :], rs[:, 3, :], 1.0 / C, EPS, ALU.mult, ALU.add).then_inc(flag, 1)

            def norm_last(src_flag, g, gain, shift, out_v, flag, extra=None):
                dve.wait_ge(src_flag, upto(src_flag, g))
                link(v.tensor_tensor(out_v[:], out_v[:], rs[:, 2, :].unsqueeze(2).to_broadcast([HALF, 8, C]), ALU.mult))
                link(v.tensor_tensor(out_v[:], out_v[:], rep[:, gain], ALU.mult))
                if extra is None:
                    v.tensor_tensor(out_v[:], out_v[:], rep[:, shift], ALU.add).then_inc(flag, 1)
                else:
                    link(v.tensor_tensor(out_v[:], out_v[:], rep[:, shift], ALU.add))
                    v.tensor_tensor(out_v[:], out_v[:], extra[:], ALU.add).then_inc(flag, 1)

            def unit_back(g, n):
                c, k, nr = n // 2, n % 2, ROWS[n]
                dve.wait_ge(rt_tr, upto(rt_tr, g, n))
                dve.wait_ge(wgt_ok, upto(wgt_ok, g, n))
                if k == 0:
                    if c >= 2:
                        dve.wait_ge(out_w[c % 2], upto(out_w[c % 2], g, c // 2 - 1))
                    else:
                        if g >= 1:
                            dve.wait_ge(out_w[c % 2], upto(out_w[c % 2], g - 1))
                v.scalar_tensor_tensor(res[:, c % 2, 4 * k * H:(4 * k + nr) * H], tr[:, n % 2, 0:nr * H],
                                                   mom[:, g, 0:1], wgt[:, n % 2, 0:nr * H], op0=ALU.subtract, op1=ALU.mult).then_inc(res_ok, 1)

            def back(g, key):
                if g >= 0:
                    for n in C_AFTER[key]:
                        unit_back(g, n)

            post(v.memset(ms[:], 0.0))
            for w in (w_conv, wq, wk, wv, wo, w1, w2, y7, vpad, zrow):
                post(v.memset(w[:], 0.0))
            post(v.memset(cvr[:], 0.0))
            post(v.memset(eps_col[:, 0:1], -0.5))
            post(v.memset(eps_col[:, 1:2], 1.0))
            sync()
            v.memset(vpad[:, :, :, HD:HD + 1], 1.0).then_inc(dve_set, 1)
            all_ready(dve)
            for b in range(NB):
                q = slice(C * b, C * b + C)
                post(v.tensor_copy(w_conv[q, :, KS * b:KS * b + KS], w_small[q]))
            post(v.tensor_copy(blk[:], blk_f))
            post(v.tensor_copy(bones[:], bones_f))
            for b in range(NB):
                post(v.tensor_copy(cs[:, b, 110:111], row_col))
            link(v.tensor_scalar(bn[:, 7:8], bn[:, 4:5], EPS, None, ALU.add))
            link(v.tensor_scalar(bn[:, 6:7], bn[:, 0:1], bn[:, 3:4], None, ALU.subtract))
            v.memset(rs[:], 0.0).then_inc(dve_set, 1)
            dve.wait_ge(bn_rstd, upto(bn_rstd, 0))
            link(v.tensor_tensor(bn[:, 5:6], bn[:, 1:2], bn[:, 7:8], ALU.mult))
            link(v.tensor_scalar(bn[:, 6:7], bn[:, 6:7], bn[:, 5:6], bn[:, 2:3], ALU.mult, ALU.add))
            for n in range(25):
                piece(0, n)
            moments(0)
            for s in range(G + 2):
                now, topk, ahead, end = s, s - 1, s + 1, s - 2
                if 0 <= topk < G:
                    topk_first(topk)
                for n in range(TOPK_STEPS):
                    if ahead < G:
                        piece(ahead, n)
                    if 0 <= topk < G:
                        refine(topk, n)
                        if n + 1 < TOPK_STEPS:
                            count(topk, n + 1)
                if ahead < G:
                    moments(ahead)
                if 0 <= topk < G:
                    find(topk)
                if now < G:
                    importance_sum(now)
                back(end, "idx")
                if 0 <= topk < G:
                    embed(topk)
                if now < G:
                    importance(now)
                back(end, "tok")
                if 0 <= topk < G:
                    soft(topk, 0)
                for n in range(8):
                    if 0 <= topk < G:
                        if n < 7:
                            soft(topk, n + 1)
                        attend(topk, n)
                    back(end, ("att", n))
                if 0 <= topk < G:
                    norm_first(wo_ok, topk, 1, tok, ra, v1_ok)
                    norm_last(r1_ok, topk, 2, 3, ra, t1_ok)
                back(end, "post1")
                if 0 <= topk < G:
                    norm_first(ff_ok, topk, 4, ra, rb, v2_ok)
                    norm_last(r2_ok, topk, 5, 6, rb, t2_ok, tok_x)
                back(end, "post2")


def constants(H, C, NB, NH, K):
    import numpy as np

    def wide(a):
        a = np.asarray(a, np.float32)
        return np.concatenate([a, np.zeros((128 - a.shape[0], a.shape[1]), np.float32)])

    p = np.arange(128)
    rows = np.arange(H)
    c100 = np.arange(100)
    slots = np.arange(96)
    return np.concatenate([wide(a) for a in (
        np.eye(128), np.ones((128, 128)), rows[:, None] < rows[None, :], c100[:, None] // 25 == c100[None, :] // 25,
        (p[:, None] // (C // NH)) == np.arange(NB * NH)[None, :], np.tile(np.arange(K), (H, 1)),
        np.stack([slots, slots + 96], 1), rows[:, None], c100[:, None] == 25 * np.arange(NB)[None, :],
        np.tile(np.tile(np.arange(NB), 2), (96, 1)), np.tile(np.tile(np.arange(NB), 2) * H * H, (96, 1)),
        np.arange(12)[:, None] % NB == p[None, :] // C,
    )], axis=1).astype(np.float32)


def positions(seq_len, dim):
    import numpy as np
    pos = np.arange(seq_len, dtype=np.float32)[:, None]
    div = np.exp(np.arange(0, dim, 2, dtype=np.float32) * -(np.log(10000.0) / dim))
    pe = np.zeros((seq_len, dim), dtype=np.float32)
    pe[:, 0::2] = np.sin(pos * div)
    pe[:, 1::2] = np.cos(pos * div)
    return pe


def kernel(**inputs):
    import numpy as np
    import concourse.bacc as bacc
    from concourse import mybir
    from concourse.bass_utils import run_bass_kernel_spmd

    a = {k.removeprefix("L0_conv_"): np.asarray(v) for k, v in inputs.items()}
    B, C, H, _ = a["x"].shape
    arrays = {
        "in_x": a["x"],
        "in_conv_w": a["conv_w"][0].transpose(0, 2, 1),
        "in_conv_b": a["conv_b"], "in_bn_g": a["bn_g"], "in_bn_b": a["bn_b"], "in_bn_m": a["bn_m"], "in_bn_v": a["bn_v"],
        "in_w_qkvT": a["w_qkv"].T, "in_b_qkv": a["b_qkv"], "in_w_oT": a["w_o"].T, "in_b_o": a["b_o"],
        "in_ln1_g": a["ln1_g"], "in_ln1_b": a["ln1_b"], "in_w1T": a["w1"].T, "in_b1": a["b1"],
        "in_w2T": a["w2"].T, "in_b2": a["b2"], "in_ln2_g": a["ln2_g"], "in_ln2_b": a["ln2_b"],
        "in_pos": positions(H * H, C), "in_const": constants(H, C, 128 // C, 8, 192),
    }
    arrays = {k: np.ascontiguousarray(v) for k, v in arrays.items()}
    nc = bacc.Bacc("TRN2", target_bir_lowering=False, num_devices=1)
    args = [nc.dram_tensor(k, v.shape, mybir.dt.from_np(v.dtype), kind="ExternalInput").ap() for k, v in arrays.items()]
    out = nc.dram_tensor("out", a["x"].shape, mybir.dt.float32, kind="ExternalOutput").ap()
    preact_conv_token_attention(nc, *args, out)
    r = run_bass_kernel_spmd(nc, [arrays], core_ids=[0])
    return r.results[0]["out"]
```

```python
import concourse.bass as bass
from concourse import mybir
from contextlib import ExitStack


def preact_conv_token_attention(
    nc, x, conv_w, conv_b, bn_g, bn_b, bn_m, bn_v, w_qkvT, b_qkv, w_oT, b_o, ln1_g, ln1_b,
    w1T, b1, w2T, b2, ln2_g, ln2_b, pos, const, out,
):
    f32, bf16, fp16, u32 = mybir.dt.float32, mybir.dt.bfloat16, mybir.dt.float16, mybir.dt.uint32
    ALU, ACT, AX = mybir.AluOpType, mybir.ActivationFunctionType, mybir.AxisListType.X

    B, C, H, _ = x.shape
    HW = H * H
    NB = 128 // C
    G = B // NB
    NH, HD = 8, C // 8
    K, HALF = 192, 96
    KS, DIL = 7, 5
    U = 28
    ROWS = [4] * 27 + [2]
    TABLES = 6
    XC, XROWS = 5, H // 5
    FCH, FL = 25, HW // 25
    EPS = 1e-5
    TOPK_STEPS = 25

    table = [nc.dram_tensor(f"table{n}", [HW * NB, C], f32).ap() for n in range(TABLES)]
    table_jt = [t.rearrange("(j i b) c -> j i (b c)", j=H, b=NB) for t in table]
    conv_rows = nc.dram_tensor("conv_rows", [NB * KS, 7, 16, H], f32).ap()
    imp_flat = [nc.dram_tensor(f"imp_flat{n}", [NB * HW, 1], f32).ap() for n in range(2)]
    parts_dram = nc.dram_tensor("parts_dram", [G, 3, NB, H, H], bf16).ap()

    ctx = ExitStack()
    with ctx:
        def sb(name, shape, dt=f32):
            return ctx.enter_context(nc.sbuf_tensor(name, shape, dt))

        def pb(name, shape, dt=f32):
            return ctx.enter_context(nc.psum_tensor(name, shape, dt))

        counted = {}

        def raised(name, per=1, step=1):
            s = ctx.enter_context(nc.semaphore(name))
            counted[s.name] = per, step
            return s

        def upto(s, g, k=None):
            per, step = counted[s.name]
            return step * (per * g + (per if k is None else k + 1))

        NCONST = const.shape[1]
        cst = sb("cst", [128, NCONST])
        at = [0]

        def take(p, n):
            v = cst[0:p, at[0]:at[0] + n]
            at[0] += n
            return v

        ident = take(128, 128)
        ones = take(128, 128)
        tri = take(H, H)
        blk_f = take(100, 100)
        head_mask = take(128, NB * NH)
        iota_k = take(H, K)
        slot_col = take(HALF, 2)
        row_col = take(H, 1)
        first_chunk = take(100, NB)
        tab_base = take(HALF, 8)
        imp_base = take(HALF, 8)
        bones_f = take(12, 128)
        blk = sb("blk", [100, 100], fp16)
        bones = sb("bones", [12, 128], bf16)
        zrow = sb("zrow", [H, H])

        w_conv = sb("w_conv", [128, KS, 32])
        w_small = sb("w_small", [128, KS, KS])
        wq = sb("wq", [128, 128])
        wk = sb("wk", [128, 128])
        wv = sb("wv", [128, 128])
        wo = sb("wo", [128, 128])
        w1 = sb("w1", [128, 2, 128])
        w2 = sb("w2", [128, 64])
        qk_bias = sb("qk_bias", [128, 2])
        b1_col = sb("b1_col", [128, 1])
        rep = sb("rep", [HALF, 7, NB, C])
        bn = sb("bn", [H, 8])
        eps_col = sb("eps_col", [128, 2])

        X = [sb(f"X{p}", [128, H, H]) for p in range(2)]
        xt = sb("xt", [H, 2, 4, 128])
        rt = sb("rt", [H, 4, 4, 128])
        imp_b = sb("imp_b", [12, 4, 4 * H], bf16)
        wgt = sb("wgt", [128, 4 * H])
        res = sb("res", [128, 2, 4 * H])
        stats = sb("stats", [128, 25, 6])
        mom = sb("mom", [128, G, 6])
        cvr = sb("cvr", [128, 2, 4 * H])
        y7 = sb("y7", [H, NB, KS, H])
        yy = sb("yy", [H, NB, H])
        ge = sb("ge", [H, NB, H])
        imp = sb("imp", [H, NB, H])
        flat = sb("flat", [100, FL])
        junk = sb("junk", [100, FL], bf16)
        th = sb("th", [100, 4])
        cnt = sb("cnt", [100, 1], fp16)
        tsel = sb("tsel", [100, NB])
        tb = sb("tb", [H, NB])
        gt = sb("gt", [H, NB, H], bf16)
        eq = sb("eq", [H, NB, H], bf16)
        cg = sb("cg", [H, NB, H], bf16)
        ce = sb("ce", [H, NB, H])
        tot = sb("tot", [H, 8])
        off = sb("off", [H, 16])
        startend = sb("startend", [H, 2 * NB])
        cs = sb("cs", [H, NB, 112], bf16)
        hot_a = sb("hot_a", [H, NB, K], bf16)
        hot = sb("hot", [H, NB, K], bf16)
        im = ce
        parts = sb("parts", [H, 3, NB, H], bf16)
        jcol = yy[0:HALF].rearrange("p b j -> p (b j)").bitcast(bf16).rearrange("p (k j) -> p k j", j=H)
        col = sb("col", [HALF, 8])
        pixf = sb("pixf", [HALF, 3, 8])
        idx = sb("idx", [HALF, 2, 3, 8], u32)
        tok_x = sb("tok_x", [HALF, 2, 8, C])
        tok_pos = sb("tok_pos", [HALF, 8, C])
        tok_imp = sb("tok_imp", [HALF, 8])
        diag = sb("diag", [128, 256])
        tok = sb("tok", [HALF, 8, C])
        tok_t = sb("tok_t", [128, K])
        q_t = sb("q_t", [128, K])
        k_t = sb("k_t", [128, K])
        vpad = sb("vpad", [HALF, 2, NB * NH, 8])
        qm = sb("qm", [128, NH, K])
        pr = sb("pr", [HALF, 2, NH, K])
        least = sb("least", [HALF, 2, 2])
        pt = sb("pt", [HALF, 2, 2, NH, HALF])
        o_t = sb("o_t", [128, 2, HALF])
        rden = sb("rden", [HALF, 2, 4])
        o_tok = sb("o_tok", [HALF, 2, NB, C])
        act_t = q_t
        hid = qm[:, 0:2]
        sq = diag[0:HALF].rearrange("p (k c) -> p k c", c=C)
        ra = sb("ra", [HALF, 8, C])
        rb = sb("rb", [HALF, 8, C])
        rs = sb("rs", [HALF, 4, 8])

        cv = pb("cv", [128, 512])
        xb = pb("xb", [128, 512])
        tr = pb("tr", [128, 512])
        ib = pb("ib", [128, 512])
        sc = pb("sc", [128, 2, 512])
        pp = pb("pp", [128, 512])
        ms = pb("ms", [128, 512])
        COUNT, OFFS, TOTS, THR = 440, 468, 476, 484

        ready = raised("ready", 1, 16)
        dve_set = raised("dve_set", 2)
        bn_rstd = raised("bn_rstd")
        x_in = [[raised(f"x_in{p}_{c}", 1, 16) for c in range(XC)] for p in range(2)]
        xt_tr = raised("xt_tr", U)
        xt_cp = raised("xt_cp", U)
        tab_w = [raised(f"tab_w{i}", U // 2, 16) for i in range(2)]
        var_ok = raised("var_ok")
        rstd_ok = raised("rstd_ok")
        xn_ok = raised("xn_ok", XC)
        conv_ok = raised("conv_ok", 7)
        cv_cp = raised("cv_cp", 7)
        cv_w = [raised(f"cv_w{i}", [4, 3][i], 64) for i in range(2)]
        y7_in = raised("y7_in", 1, 16 * KS)
        y_ok = raised("y_ok", 2)
        gelu_ok = raised("gelu_ok")
        imp_ok = raised("imp_ok", 2)
        imp_w = raised("imp_w", 1, 16)
        flat_in = raised("flat_in", 1, 16)
        imp_in = raised("imp_in", 1, 16)
        cnt_ok = raised("cnt_ok", TOPK_STEPS)
        cnt_sum = raised("cnt_sum", TOPK_STEPS)
        small_rd = raised("small_rd", TOPK_STEPS + 2)
        tsel_ok = raised("tsel_ok")
        tb_ok = raised("tb_ok")
        tot_ok = raised("tot_ok")
        off_ok = raised("off_ok")
        hot_ok = raised("hot_ok")
        pick_ok = raised("pick_ok")
        im_ok = raised("im_ok")
        part_ok = raised("part_ok")
        parts_w = raised("parts_w", 1, 16)
        idx_ok = raised("idx_ok")
        tok_in = raised("tok_in", 1, 24 * 16)
        diag_ok = raised("diag_ok")
        rep_ok = raised("rep_ok")
        tok_ok = raised("tok_ok")
        tokt_ok = raised("tokt_ok")
        tokt_cp = raised("tokt_cp")
        qkv_ok = raised("qkv_ok")
        qk_cp = raised("qk_cp", 2)
        v_cp = raised("v_cp")
        qm_ok = raised("qm_ok", 4 * NB)
        s_ok = raised("s_ok", 32)
        least_ok = raised("least_ok", 32)
        e_ok = raised("e_ok", 32)
        pt_tr = raised("pt_tr", 32)
        pt_cp = raised("pt_cp", 32)
        pv_ok = raised("pv_ok", 8)
        ot_cp = raised("ot_cp", 8)
        ot_tr = raised("ot_tr", 8)
        o_ok = raised("o_ok", 8)
        oa_tr = raised("oa_tr")
        oa_cp = raised("oa_cp")
        wo_ok = raised("wo_ok")
        v1_ok = raised("v1_ok")
        r1_ok = raised("r1_ok")
        t1_ok = raised("t1_ok")
        t1_tr = raised("t1_tr")
        t1_cp = raised("t1_cp")
        h_ok = raised("h_ok")
        h_cp = raised("h_cp")
        ff_ok = raised("ff_ok")
        v2_ok = raised("v2_ok")
        r2_ok = raised("r2_ok")
        t2_ok = raised("t2_ok")
        scat = raised("scat", 1, 8 * 16)
        rt_in = [raised(f"rt_in{i}", U // 4, 16) for i in range(4)]
        ib_in = [raised(f"ib_in{i}", U // 4, 16) for i in range(4)]
        rt_tr = raised("rt_tr", U)
        ib_ok = raised("ib_ok", U)
        wgt_ok = raised("wgt_ok", U)
        res_ok = raised("res_ok", U)
        fin_ok = raised("fin_ok", U)
        out_w = [raised(f"out_w{i}", U // 2, 16) for i in range(2)]
        own = {e: ctx.enter_context(nc.semaphore(f"own_{e}")) for e in ("dve", "act", "pool")}

        block = ctx.enter_context(nc.Block())

        LOAD, INTO, NORMAL = -28, -23, (-8, -4, 0, 4, 8)
        TAPS, SUM, GELU, IMP_OUT, FLAT = 29, 31, 33, 36, 37
        SEARCH, IMP_IN, MASKS, RANKS, INDEX = 39, 59, 64, 65, 66
        GATHER, REST, SPLIT, PARTS_OUT = 67, 68, (70, 72, 74), 75
        EMBED, SCORES, TURN, VALUES = 76, 77, 79, 81
        MIX, FEED, SCATTER, BACK = 97, 99, 103, 107
        SLOTS = range(LOAD, U * G + BACK)

        def at(slot, first, n=1):
            g, k = (slot - first) // U, (slot - first) % U
            return [(g, k)] if k < n and 0 <= g < G else []

        loads = [0]

        @block.sync
        def _(sp):
            def load(dst, src):
                sp.dma_start(dst, src).then_inc(ready, 16)
                loads[0] += 1

            def load_x(g, c):
                if g >= 2 and c == 0:
                    sp.wait_ge(conv_ok, upto(conv_ok, g - 2))
                xs = x.rearrange("(g b) c h w -> g (b c) h w", b=NB)[g]
                r = slice(c * XROWS, (c + 1) * XROWS)
                sp.dma_start(X[g % 2][:, r, :], xs[:, r, :]).then_inc(x_in[g % 2][c], 16)

            load(cst[:], const)
            for c in range(XC):
                load_x(0, c)
            for b in range(NB):
                load(w_small[C * b:C * b + C], conv_w)
            sp.wait_ge(dve_set, upto(dve_set, 0, 0))
            for b in range(NB):
                q = slice(C * b, C * b + C)
                for n, w in enumerate((wq, wk, wv)):
                    load(w[q, q], w_qkvT[:, n * C:(n + 1) * C])
                load(wo[q, q], w_oT)
                load(w1[q, b // 2, 64 * (b % 2):64 * (b % 2) + 64], w1T)
                for n in range(2):
                    load(qk_bias[q, n:n + 1], b_qkv[n * C:(n + 1) * C].rearrange("(c o) -> c o", o=1))
            for b in range(2):
                load(w2[64 * b:64 * b + 64, C * b:C * b + C], w2T)
                load(b1_col[64 * b:64 * b + 64, :], b1.rearrange("(c o) -> c o", o=1))
            for n, v in enumerate((b_qkv[2 * C:3 * C], b_o, ln1_g, ln1_b, b2, ln2_g, ln2_b)):
                load(rep[:, n], v.rearrange("(o p c) -> o p c", o=1, p=1).broadcast_to([HALF, NB, C]))
            for n, v in enumerate((conv_b, bn_g, bn_b, bn_m, bn_v)):
                load(bn[:, n:n + 1], v.rearrange("(o c) -> o c", o=1).broadcast_to([H, 1]))
            for c in range(XC):
                load_x(1, c)

            def table_out(g, u):
                if u == 0 and g >= TABLES:
                    for i in range(4):
                        sp.wait_ge(rt_in[i], upto(rt_in[i], g - TABLES))
                sp.wait_ge(xt_cp, upto(xt_cp, g, u))
                sp.dma_start(table_jt[g % TABLES][:, 4 * u:4 * u + ROWS[u], :], xt[:, u % 2, 0:ROWS[u], :]).then_inc(tab_w[u % 2], 16)

            def back_in(g, u):
                if u == 0:
                    sp.wait_ge(scat, upto(scat, g))
                    sp.wait_ge(parts_w, upto(parts_w, g))
                if u >= 4:
                    sp.wait_ge(rt_tr, upto(rt_tr, g, u - 4))
                    sp.wait_ge(ib_ok, upto(ib_ok, g, u - 4))
                elif g >= 1:
                    sp.wait_ge(rt_tr, upto(rt_tr, g - 1, U - 4 + u))
                    sp.wait_ge(ib_ok, upto(ib_ok, g - 1, U - 4 + u))
                nr = ROWS[u]
                sp.dma_start(rt[:, u % 4, 0:nr, :], table_jt[g % TABLES][:, 4 * u:4 * u + nr, :]).then_inc(rt_in[u % 4], 16)
                sp.dma_start(imp_b[:, u % 4, 0:nr * H],
                             parts_dram[g, :, :, 4 * u:4 * u + nr, :].rearrange("q b i j -> (q b) (i j)")
                             ).then_inc(ib_in[u % 4], 16)

            def out_store(g, u):
                sp.wait_ge(fin_ok, upto(fin_ok, g, u))
                og = out.rearrange("(g b) c h w -> g (b c) h w", b=NB)[g]
                nr = ROWS[u]
                sp.dma_start(og[:, 4 * u:4 * u + nr, :].rearrange("p i j -> p (i j)"),
                             res[:, u % 2, 0:nr * H]).then_inc(out_w[u % 2], 16)

            def round_out(g, t):
                sp.wait_ge(cv_cp, upto(cv_cp, g, t))
                if t == 0 and g:
                    sp.wait_ge(y7_in, upto(y7_in, g - 1))
                for q in range(4):
                    sp.dma_start(conv_rows[:, t, 4 * q:4 * q + 4, :].rearrange("p r j -> p (r j)"),
                                 cvr[32 * q:32 * q + NB * KS, t % 2, :]).then_inc(cv_w[t % 2], 16)

            def taps_in(g):
                for i in range(2):
                    sp.wait_ge(cv_w[i], upto(cv_w[i], g))
                if g:
                    sp.wait_ge(y_ok, upto(y_ok, g - 1))
                rows = conv_rows.rearrange("(b k) t r j -> k (t r) b j", k=KS)
                for ki in range(KS):
                    o = DIL * (ki - 3)
                    i0, i1 = max(0, -o), min(H, H - o)
                    sp.dma_start(y7[i0:i1, :, ki, :], rows[ki, i0 + o:i1 + o, :, :]).then_inc(y7_in, 16)

            def imp_out(g):
                sp.wait_ge(imp_ok, upto(imp_ok, g))
                if g >= 2:
                    sp.wait_ge(tok_in, upto(tok_in, g - 2))
                    sp.wait_ge(imp_in, upto(imp_in, g - 2))
                sp.dma_start(imp_flat[g % 2].rearrange("(b i j) o -> i b (j o)", b=NB, i=H), ge[:]).then_inc(imp_w, 16)

            def flat_load(g):
                sp.wait_ge(imp_w, upto(imp_w, g))
                if g:
                    sp.wait_ge(cnt_ok, upto(cnt_ok, g - 1))
                sp.dma_start(flat[:], imp_flat[g % 2].rearrange("(p f) o -> p (f o)", f=FL)).then_inc(flat_in, 16)

            def imp_load(g):
                if g:
                    sp.wait_ge(im_ok, upto(im_ok, g - 1))
                sp.dma_start(imp[:], imp_flat[g % 2].rearrange("(b i j) o -> i b (j o)", b=NB, i=H)).then_inc(imp_in, 16)

            def parts_out(g):
                sp.wait_ge(part_ok, upto(part_ok, g))
                sp.dma_start(parts_dram[g].rearrange("q b i j -> i (q b) j"),
                             parts[:].rearrange("p q b j -> p (q b) j")).then_inc(parts_w, 16)

            for s in SLOTS:
                for g, n in at(s, LOAD, XC):
                    if g >= 2:
                        load_x(g, n)
                for g, n in at(s, INTO, 14):
                    table_out(g, 2 * n)
                for g, n in at(s, 3, 25):
                    if n % 4 == 0:
                        round_out(g, n // 4)
                for g, n in at(s, BACK - 2):
                    for u in range(4):
                        back_in(g, u)
                for g, n in at(s, BACK + 1, U - 4):
                    back_in(g, n + 4)
                for g, n in at(s, INTO, 14):
                    table_out(g, 2 * n + 1)
                for g, n in at(s, BACK, U):
                    out_store(g, n)
                for g, n in at(s, TAPS):
                    taps_in(g)
                for g, n in at(s, IMP_OUT):
                    imp_out(g)
                for g, n in at(s, FLAT):
                    flat_load(g)
                for g, n in at(s, IMP_IN):
                    imp_load(g)
                for g, n in at(s, PARTS_OUT):
                    parts_out(g)
            for i in range(2):
                sp.wait_ge(out_w[i], upto(out_w[i], G - 1))

        NL = loads[0]

        @block.tensor
        def _(pe):
            mm = nc.tensor.matmul

            def unit_in(g, u):
                for c in range(XC):
                    if 4 * (u - 1) + 3 < c * XROWS <= 4 * u + ROWS[u] - 1:
                        pe.wait_ge(x_in[g % 2][c], upto(x_in[g % 2][c], g // 2))
                if u:
                    pe.wait_ge(xt_cp, upto(xt_cp, g, u - 1))
                elif g:
                    pe.wait_ge(xt_cp, upto(xt_cp, g - 1))
                for r in range(ROWS[u]):
                    last = nc.tensor.transpose(xb[0:H, 128 * r:128 * r + 128], X[g % 2][:, 4 * u + r, :], ident)
                last.then_inc(xt_tr, 1)

            def conv_part(g, n):
                t, part = n // 4, n % 4
                for c in range(XC):
                    if part == 0 and 16 * t - 1 < c * XROWS <= 16 * t + 15:
                        pe.wait_ge(xn_ok, upto(xn_ok, g, c))
                if part == 0:
                    if t:
                        pe.wait_ge(cv_cp, upto(cv_cp, g, t - 1))
                    elif g:
                        pe.wait_ge(cv_cp, upto(cv_cp, g - 1))
                order = [3, 0, 1, 2, 4, 5, 6]
                for m in range(7 * part, 7 * part + 7):
                    kj, q = order[m // 4], m % 4
                    u = 4 * t + q
                    shift, nr = DIL * (kj - 3), ROWS[u]
                    j0, j1 = max(0, -shift), min(H, H - shift)
                    o = cv[32 * q:32 * q + 32, 0:nr * H].rearrange("p (r j) -> p r j", j=H)
                    last = mm(o[:, :, j0:j1], w_conv[:, kj, :], X[g % 2][:, 4 * u:4 * u + nr, j0 + shift:j1 + shift],
                              start=m < 4, stop=m >= 24, skip_group_check=True)
                if part == 3:
                    last.then_inc(conv_ok, 1)

            searched, backed = [], []

            def count(g, k):
                for value in backed[-1:]:
                    pe.wait_ge(res_ok, value)
                pe.wait_ge(cnt_ok, upto(cnt_ok, g, k))
                mm(tr[0:100, COUNT + k:COUNT + k + 1], blk[:], cnt[:], start=True, stop=True).then_inc(cnt_sum, 1)
                searched.append(upto(small_rd, g, k))

            def unit_back(g, u):
                nr = ROWS[u]
                for value in backed[-1:]:
                    pe.wait_ge(res_ok, value)
                for value in searched[-1:]:
                    pe.wait_ge(small_rd, value)
                backed.append(upto(res_ok, g, u))
                pe.wait_ge(rt_in[u % 4], upto(rt_in[u % 4], g, u // 4))
                for r in range(nr):
                    last = nc.tensor.transpose(tr[:, H * r:H * r + H], rt[:, u % 4, r, :], ident[0:H, 0:H])
                last.then_inc(rt_tr, 1)

            def spread(g, u):
                nr = ROWS[u]
                pe.wait_ge(ib_in[u % 4], upto(ib_in[u % 4], g, u // 4))
                if u:
                    pe.wait_ge(wgt_ok, upto(wgt_ok, g, u - 1))
                elif g:
                    pe.wait_ge(wgt_ok, upto(wgt_ok, g - 1))
                mm(ib[:, 0:nr * H], bones[:], imp_b[:, u % 4, 0:nr * H], start=True, stop=True).then_inc(ib_ok, 1)

            def thresholds(g):
                for value in backed[-1:]:
                    pe.wait_ge(res_ok, value)
                searched.append(upto(small_rd, g, TOPK_STEPS))
                pe.wait_ge(tsel_ok, upto(tsel_ok, g))
                mm(tr[0:H, THR:THR + NB], ones[0:100, 0:H], tsel[:], start=True, stop=True).then_inc(tb_ok, 1)

            def offsets(g):
                for value in backed[-1:]:
                    pe.wait_ge(res_ok, value)
                searched.append(upto(small_rd, g))
                pe.wait_ge(tot_ok, upto(tot_ok, g))
                mm(tr[0:H, OFFS:OFFS + 8], tri, tot[:], start=True, stop=True)
                mm(tr[0:H, TOTS:TOTS + 8], ones[0:H, 0:H], tot[:], start=True, stop=True).then_inc(off_ok, 1)

            def pick(g):
                pe.wait_ge(hot_ok, upto(hot_ok, g))
                if g >= 1:
                    pe.wait_ge(e_ok, upto(e_ok, g - 1))
                for half in range(2):
                    for b in range(NB):
                        last = mm(sc[0:HALF, half, 112 * b:112 * b + 111], hot[:, b, HALF * half:HALF * half + HALF],
                                  cs[:, b, 0:111], start=True, stop=True)
                last.then_inc(pick_ok, 1)

            def embed(g):
                pe.wait_ge(diag_ok, upto(diag_ok, g))
                mm(ms[0:HALF, 0:256], ones[:, 0:HALF], diag[:], start=True, stop=True).then_inc(rep_ok, 1)
                pe.wait_ge(tok_ok, upto(tok_ok, g))
                for half in range(2):
                    last = nc.tensor.transpose(pp[:, HALF * half:HALF * half + HALF],
                                               tok[:, NB * half:NB * half + NB, :].rearrange("p b c -> p (b c)"), ident[0:HALF, 0:HALF])
                last.then_inc(tokt_ok, 1)
                pe.wait_ge(tokt_cp, upto(tokt_cp, g))
                mm(sc[:, 0, 0:K], wq[:], tok_t[:], start=True, stop=True)
                mm(sc[:, 1, 0:K], wk[:], tok_t[:], start=True, stop=True)
                for half in range(2):
                    last = mm(ms[0:HALF, 128 * half:128 * half + 128], tok_t[:, HALF * half:HALF * half + HALF], wv[:],
                              start=True, stop=True)
                last.then_inc(qkv_ok, 1)

            def scores(g, k):
                b, half, pair = k // 8, (k // 4) % 2, k % 4
                if k == 0:
                    pe.wait_ge(qk_cp, upto(qk_cp, g))
                if half == 0:
                    pe.wait_ge(qm_ok, upto(qm_ok, g, 4 * b + pair))
                if k >= 2:
                    pe.wait_ge(e_ok, upto(e_ok, g, k - 2))
                for h in range(2):
                    last = mm(sc[0:HALF, k % 2, K * h:K * h + K], qm[:, 2 * pair + h, HALF * half:HALF * half + HALF],
                              k_t[:], start=True, stop=True)
                last.then_inc(s_ok, 1)

            def turn(g, k):
                unit, kh, hg = k // 4, (k // 2) % 2, k % 2
                if k % 4 == 0:
                    pe.wait_ge(e_ok, upto(e_ok, g, 4 * unit + 3))
                if k:
                    pe.wait_ge(pt_cp, upto(pt_cp, g, k - 1))
                for h in range(4):
                    last = nc.tensor.transpose(pp[0:HALF, HALF * h:HALF * h + HALF],
                                               pr[:, unit % 2, 4 * hg + h, HALF * kh:HALF * kh + HALF], ident[0:HALF, 0:HALF])
                last.then_inc(pt_tr, 1)

            def values(g, unit):
                b = unit // 2
                if unit == 0:
                    pe.wait_ge(v_cp, upto(v_cp, g))
                else:
                    pe.wait_ge(o_ok, upto(o_ok, g, unit - 1))
                pe.wait_ge(pt_cp, upto(pt_cp, g, 4 * unit + 3))
                for hh in range(2):
                    for kh in range(2):
                        for q in range(4):
                            h = 4 * hh + q
                            last = mm(ms[32 * q:32 * q + 8, HALF * hh:HALF * hh + HALF], vpad[:, kh, NH * b + h, :],
                                      pt[:, unit % 2, kh, h, :], start=kh == 0, stop=kh == 1, skip_group_check=True)
                last.then_inc(pv_ok, 1)

            def values_turn(g, unit):
                pe.wait_ge(ot_cp, upto(ot_cp, g, unit))
                for hh in range(2):
                    last = nc.tensor.transpose(ms[0:HALF, 256 + 128 * hh:384 + 128 * hh], o_t[:, hh, :], ident)
                last.then_inc(ot_tr, 1)

            def mix(g):
                pe.wait_ge(o_ok, upto(o_ok, g))
                for half in range(2):
                    last = nc.tensor.transpose(pp[:, HALF * half:HALF * half + HALF],
                                               o_tok[:, half].rearrange("p b c -> p (b c)"), ident[0:HALF, 0:HALF])
                last.then_inc(oa_tr, 1)
                pe.wait_ge(oa_cp, upto(oa_cp, g))
                for half in range(2):
                    last = mm(ms[0:HALF, 128 * half:128 * half + 128], act_t[:, HALF * half:HALF * half + HALF], wo[:],
                              start=True, stop=True)
                last.then_inc(wo_ok, 1)

            def feed(g):
                pe.wait_ge(t1_ok, upto(t1_ok, g))
                for half in range(2):
                    last = nc.tensor.transpose(pp[:, HALF * half:HALF * half + HALF],
                                               ra[:, NB * half:NB * half + NB, :].rearrange("p b c -> p (b c)"), ident[0:HALF, 0:HALF])
                last.then_inc(t1_tr, 1)
                pe.wait_ge(t1_cp, upto(t1_cp, g))
                for pair in range(2):
                    last = mm(sc[:, 0, K * pair:K * pair + K], w1[:, pair, :], act_t[:], start=True, stop=True)
                last.then_inc(h_ok, 1)

            def feed_last(g):
                pe.wait_ge(h_cp, upto(h_cp, g))
                for half in range(2):
                    for pair in range(2):
                        last = mm(ms[0:HALF, 128 * half + 64 * pair:128 * half + 64 * pair + 64],
                                  hid[:, pair, HALF * half:HALF * half + HALF], w2[:], start=True, stop=True)
                last.then_inc(ff_ok, 1)

            pe.wait_ge(ready, 16 * NL)
            pe.wait_ge(dve_set, upto(dve_set, 0))
            for s in SLOTS:
                for g, n in at(s, INTO, 14):
                    unit_in(g, 2 * n)
                for g, n in at(s, BACK, U):
                    unit_back(g, n)
                for g, n in at(s, 0, U):
                    conv_part(g, n)
                for g, n in at(s, SCORES, 16):
                    scores(g, 2 * n)
                for g, n in at(s, TURN, 16):
                    turn(g, 2 * n)
                for g, n in at(s, BACK - 1, U):
                    spread(g, n)
                for g, n in at(s, SEARCH, TOPK_STEPS):
                    count(g, n)
                for g, n in at(s, INTO, 14):
                    unit_in(g, 2 * n + 1)
                for g, n in at(s, SCORES, 16):
                    scores(g, 2 * n + 1)
                for g, n in at(s, TURN, 16):
                    turn(g, 2 * n + 1)
                for g, n in at(s, VALUES, 16):
                    (values_turn if n % 2 else values)(g, n // 2)
                for g, n in at(s, MASKS):
                    thresholds(g)
                for g, n in at(s, RANKS):
                    offsets(g)
                    pick(g)
                for g, n in at(s, MIX):
                    mix(g)
                for g, n in at(s, FEED):
                    feed(g)
                for g, n in at(s, FEED + 1):
                    feed_last(g)
                for g, n in at(s, EMBED):
                    embed(g)

        @block.scalar
        def _(act):
            mine = [0]
            A = nc.scalar.activation

            def link(ins):
                mine[0] += 1
                ins.then_inc(own["act"], 1)
                act.wait_ge(own["act"], mine[0])

            def unit_in(g, u):
                act.wait_ge(xt_tr, upto(xt_tr, g, u))
                if u >= 2:
                    act.wait_ge(tab_w[u % 2], upto(tab_w[u % 2], g, u // 2 - 1))
                elif g:
                    act.wait_ge(tab_w[u % 2], upto(tab_w[u % 2], g - 1))
                nr = ROWS[u]
                nc.scalar.copy(xt[:, u % 2, 0:nr, :].rearrange("p r c -> p (r c)"), xb[0:H, 0:128 * nr]).then_inc(xt_cp, 1)

            def round_copy(g, t):
                act.wait_ge(conv_ok, upto(conv_ok, g, t))
                if t >= 2:
                    act.wait_ge(cv_w[t % 2], upto(cv_w[t % 2], g, t // 2 - 1))
                elif g:
                    act.wait_ge(cv_w[t % 2], upto(cv_w[t % 2], g - 1))
                if t < 6:
                    nc.scalar.copy(cvr[:, t % 2, :], cv[:, 0:4 * H]).then_inc(cv_cp, 1)
                else:
                    link(nc.scalar.copy(cvr[96:128, 0, 0:2 * H], cv[96:128, 0:2 * H]))
                    nc.scalar.copy(cvr[0:96, 0, :], cv[0:96, 0:4 * H]).then_inc(cv_cp, 1)

            def importance(g):
                act.wait_ge(y_ok, upto(y_ok, g))
                link(A(ge[:].rearrange("p b j -> p (b j)"), yy[:].rearrange("p b j -> p (b j)"), ACT.Gelu,
                       scale=bn[:, 5:6], bias=bn[:, 6:7]))
                A(ge[:], ge[:], ACT.Exp, scale=-1.0).then_inc(gelu_ok, 1)

            def unit_back(g, u):
                act.wait_ge(ib_ok, upto(ib_ok, g, u))
                if u:
                    act.wait_ge(res_ok, upto(res_ok, g, u - 1))
                elif g:
                    act.wait_ge(res_ok, upto(res_ok, g - 1))
                A(wgt[:, 0:ROWS[u] * H], ib[:, 0:ROWS[u] * H], ACT.Identity, scale=mom[:, g, 2:3],
                  bias=eps_col[:, 1:2]).then_inc(wgt_ok, 1)

            def embed(g):
                act.wait_ge(tokt_ok, upto(tokt_ok, g))
                nc.scalar.copy(tok_t[:], pp[:, 0:K]).then_inc(tokt_cp, 1)
                act.wait_ge(qkv_ok, upto(qkv_ok, g))
                if g:
                    act.wait_ge(qm_ok, upto(qm_ok, g - 1))
                    act.wait_ge(s_ok, upto(s_ok, g - 1))
                A(q_t[:], sc[:, 0, 0:K], ACT.Identity, scale=-HD ** -0.5, bias=qk_bias[:, 0:1]).then_inc(qk_cp, 1)
                A(k_t[:], sc[:, 1, 0:K], ACT.Identity, bias=qk_bias[:, 1:2]).then_inc(qk_cp, 1)

            def exps(g, k):
                unit, pair = k // 4, k % 4
                act.wait_ge(least_ok, upto(least_ok, g, k))
                if pair == 0 and unit >= 2:
                    act.wait_ge(pt_tr, upto(pt_tr, g, 4 * (unit - 2) + 3))
                elif pair == 0 and g:
                    act.wait_ge(pt_tr, upto(pt_tr, g - 1))
                for h in range(2):
                    last = A(pr[:, unit % 2, 2 * pair + h, :], sc[0:HALF, k % 2, K * h:K * h + K], ACT.Exp,
                             scale=-1.0, bias=least[:, k % 2, h:h + 1])
                last.then_inc(e_ok, 1)

            def turn(g, k):
                unit, kh, hg = k // 4, (k // 2) % 2, k % 2
                act.wait_ge(pt_tr, upto(pt_tr, g, k))
                if k % 4 == 0 and unit >= 2:
                    act.wait_ge(pv_ok, upto(pv_ok, g, unit - 2))
                elif k % 4 == 0 and g:
                    act.wait_ge(pv_ok, upto(pv_ok, g - 1))
                nc.scalar.copy(pt[:, unit % 2, kh, 4 * hg:4 * hg + 4, :],
                               pp[0:HALF, 0:4 * HALF].rearrange("p (h q) -> p h q", q=HALF)).then_inc(pt_cp, 1)

            def values(g, unit):
                act.wait_ge(pv_ok, upto(pv_ok, g, unit))
                if unit:
                    act.wait_ge(ot_tr, upto(ot_tr, g, unit - 1))
                elif g:
                    act.wait_ge(ot_tr, upto(ot_tr, g - 1))
                nc.scalar.copy(o_t[:], ms[:, 0:2 * HALF].rearrange("p (a q) -> p a q", a=2)).then_inc(ot_cp, 1)

            def mix(g):
                act.wait_ge(oa_tr, upto(oa_tr, g))
                nc.scalar.copy(act_t[:], pp[:, 0:K]).then_inc(oa_cp, 1)

            def feed(g):
                act.wait_ge(t1_tr, upto(t1_tr, g))
                nc.scalar.copy(act_t[:], pp[:, 0:K]).then_inc(t1_cp, 1)
                act.wait_ge(h_ok, upto(h_ok, g))
                A(hid.rearrange("p a q -> p (a q)"), sc[:, 0, 0:2 * K], ACT.Relu, bias=b1_col[:]).then_inc(h_cp, 1)

            act.wait_ge(ready, 16 * NL)
            act.wait_ge(dve_set, upto(dve_set, 0))
            link(nc.scalar.mul(qk_bias[:, 0:1], qk_bias[:, 0:1], -HD ** -0.5))
            for s in SLOTS:
                for g, n in at(s, INTO, 14):
                    unit_in(g, 2 * n)
                for g, n in at(s, 0, U):
                    if n % 4 == 3:
                        round_copy(g, n // 4)
                for g, n in at(s, SCORES, 16):
                    exps(g, 2 * n)
                for g, n in at(s, TURN, 16):
                    turn(g, 2 * n)
                for g, n in at(s, GELU):
                    importance(g)
                for g, n in at(s, BACK - 1, U):
                    unit_back(g, n)
                for g, n in at(s, INTO, 14):
                    unit_in(g, 2 * n + 1)
                for g, n in at(s, SCORES, 16):
                    exps(g, 2 * n + 1)
                for g, n in at(s, TURN, 16):
                    turn(g, 2 * n + 1)
                for g, n in at(s, VALUES, 16):
                    if n % 2 == 0:
                        values(g, n // 2)
                for g, n in at(s, MIX):
                    mix(g)
                for g, n in at(s, FEED):
                    feed(g)
                for g, n in at(s, EMBED):
                    embed(g)

        @block.gpsimd
        def _(pool):
            gp = nc.gpsimd
            mine = [0]

            def link(ins):
                mine[0] += 1
                ins.then_inc(own["pool"], 1)
                pool.wait_ge(own["pool"], mine[0])

            def normalise(g, c):
                if c == 0:
                    pool.wait_ge(var_ok, upto(var_ok, g))
                    gp.tensor_tensor(mom[:, g, 2:3], mom[:, g, 4:5], eps_col[:, 0:1], ALU.pow).then_inc(rstd_ok, 1)
                    pool.wait_ge(rstd_ok, upto(rstd_ok, g))
                    pool.wait_ge(xt_tr, upto(xt_tr, g))
                v = X[g % 2][:, c * XROWS:(c + 1) * XROWS, :].rearrange("p r j -> p (r j)")
                gp.tensor_scalar(v, v, mom[:, g, 3:4], mom[:, g, 2:3], ALU.add, ALU.mult).then_inc(xn_ok, 1)

            def split(g, n):
                if n == 0:
                    pool.wait_ge(im_ok, upto(im_ok, g))
                    if g:
                        pool.wait_ge(parts_w, upto(parts_w, g - 1))
                if n < 2:
                    link(gp.tensor_copy(parts[:, n], im[:]))
                    link(gp.tensor_tensor(im[:], im[:], parts[:, n], ALU.subtract))
                else:
                    gp.tensor_copy(parts[:, 2], im[:]).then_inc(part_ok, 1)

            def gather(g, k):
                if k == 0:
                    pool.wait_ge(idx_ok, upto(idx_ok, g))
                    for i in range(2):
                        pool.wait_ge(tab_w[i], upto(tab_w[i], g))
                    pool.wait_ge(imp_w, upto(imp_w, g))
                    if g:
                        pool.wait_ge(tok_ok, upto(tok_ok, g - 1))
                    if g >= 2:
                        pool.wait_ge(t2_ok, upto(t2_ok, g - 2))
                for dst, src, n in ((tok_x[:, g % 2, k, :], table[g % TABLES], 0), (tok_imp[:, k:k + 1], imp_flat[g % 2], 1),
                                    (tok_pos[:, k, :], pos, 2)):
                    gp.indirect_dma_start(dst, None, src, bass.IndirectOffsetOnAxis(ap=idx[:, g % 2, n, k:k + 1], axis=0)
                                          ).then_inc(tok_in, 16)

            def masked(g, j):
                b, pair = j // 4, j % 4
                if j == 0:
                    pool.wait_ge(qk_cp, upto(qk_cp, g, 0))
                if b:
                    pool.wait_ge(s_ok, upto(s_ok, g, 8 * (b - 1) + 4 + pair))
                for h in range(2 * pair, 2 * pair + 2):
                    last = gp.tensor_scalar(qm[:, h, :], q_t[:], head_mask[:, NH * b + h:NH * b + h + 1], 1.0, ALU.mult, ALU.mult)
                last.then_inc(qm_ok, 1)

            def finish(g, u):
                pool.wait_ge(res_ok, upto(res_ok, g, u))
                v = res[:, u % 2, 0:ROWS[u] * H]
                gp.tensor_scalar(v, v, 1.0, mom[:, g, 0:1], ALU.mult, ALU.add).then_inc(fin_ok, 1)

            def scatter(g, part):
                pool.wait_ge(t2_ok, upto(t2_ok, g))
                for k in range(4 * part, 4 * part + 4):
                    gp.indirect_dma_start(table[g % TABLES], bass.IndirectOffsetOnAxis(ap=idx[:, g % 2, 0, k:k + 1], axis=0),
                                          rb[:, k, :], None).then_inc(scat, 16)

            pool.wait_ge(ready, 16 * NL)
            pool.wait_ge(dve_set, upto(dve_set, 0))
            gp.tensor_tensor(bn[:, 7:8], bn[:, 7:8], eps_col[0:H, 0:1], ALU.pow).then_inc(bn_rstd, 1)
            power_in = eps_col[0:HALF, 0:1].broadcast_to([HALF, 8])
            for s in SLOTS:
                for g, n in at(s, SCORES, 16):
                    if n % 4 >= 2 and n < 14:
                        for pair in (2 * (n % 2), 2 * (n % 2) + 1):
                            masked(g, n // 4 * 4 + 4 + pair)
                for g, n in at(s, BACK, U):
                    finish(g, n)
                for g, n in at(s, MIX + 1):
                    pool.wait_ge(v1_ok, upto(v1_ok, g))
                    gp.tensor_tensor(rs[:, 2, :], rs[:, 1, :], power_in, ALU.pow).then_inc(r1_ok, 1)
                for g, n in at(s, FEED + 3):
                    pool.wait_ge(v2_ok, upto(v2_ok, g))
                    gp.tensor_tensor(rs[:, 2, :], rs[:, 1, :], power_in, ALU.pow).then_inc(r2_ok, 1)
                for g, n in at(s, EMBED):
                    for j in range(4):
                        masked(g, j)
                for g, n in at(s, GATHER, 8):
                    gather(g, n)
                for g, n in at(s, SCATTER, 2):
                    scatter(g, n)
                for k in range(3):
                    for g, n in at(s, SPLIT[k]):
                        split(g, k)
                for c in range(XC):
                    for g, n in at(s, NORMAL[c]):
                        normalise(g, c)

        @block.vector
        def _(dve):
            v = nc.vector
            mine = [0]

            def post(ins):
                mine[0] += 1
                ins.then_inc(own["dve"], 1)

            def sync():
                dve.wait_ge(own["dve"], mine[0])

            def link(ins):
                post(ins)
                sync()

            def piece(g, n):
                if n >= 25:
                    return
                if n % 5 == 0:
                    dve.wait_ge(x_in[g % 2][n // 5], upto(x_in[g % 2][n // 5], g // 2))
                post(v.bn_stats(stats[:, n, :], X[g % 2][:].rearrange("p i j -> p (i j)")[:, n * FL:(n + 1) * FL]))

            def moments(g):
                sync()
                link(v.bn_aggr(mom[:, g, 0:2], stats[:].rearrange("p a b -> p (a b)")))
                link(v.tensor_scalar(mom[:, g, 3:4], mom[:, g, 0:1], -1.0, None, ALU.mult))
                v.tensor_scalar(mom[:, g, 4:5], mom[:, g, 1:2], EPS, None, ALU.add).then_inc(var_ok, 1)

            def count(g, k):
                if k == 0:
                    dve.wait_ge(flat_in, upto(flat_in, g))
                    link(v.memset(th[:, 0:1], 0.4375 + 0.5))
                v.tensor_scalar(junk[:], flat[:], th[:, 0:1], None, ALU.is_ge, ALU.add, accum_out=cnt[:]).then_inc(cnt_ok, 1)

            def refine(g, k):
                dve.wait_ge(cnt_sum, upto(cnt_sum, g, k))
                step = 2.0 ** -(k + 1)
                v.tensor_scalar(th[:, 1:2], tr[0:100, COUNT + k:COUNT + k + 1], K - 0.5, step, ALU.is_ge, ALU.mult).then_inc(small_rd, 1)
                dve.wait_ge(small_rd, upto(small_rd, g, k))
                if k < TOPK_STEPS - 2:
                    link(v.scalar_tensor_tensor(th[:, 0:1], th[:, 1:2], -step / 2, th[:, 0:1], op0=ALU.add, op1=ALU.add))
                elif k == TOPK_STEPS - 2:
                    link(v.scalar_tensor_tensor(th[:, 2:3], th[:, 1:2], -step, th[:, 0:1], op0=ALU.add, op1=ALU.add))
                    link(v.tensor_scalar(th[:, 0:1], th[:, 2:3], step / 2, None, ALU.add))
                else:
                    link(v.tensor_tensor(th[:, 3:4], th[:, 1:2], th[:, 2:3], ALU.add))

            def find_first(g):
                v.tensor_scalar(tsel[:], first_chunk, th[:, 3:4], None, ALU.mult).then_inc(tsel_ok, 1)

            def find_masks(g):
                dve.wait_ge(tb_ok, upto(tb_ok, g))
                v.tensor_copy(tb[:], tr[0:H, THR:THR + NB]).then_inc(small_rd, 1)
                dve.wait_ge(small_rd, upto(small_rd, g, TOPK_STEPS))
                dve.wait_ge(imp_in, upto(imp_in, g))
                if g:
                    dve.wait_ge(part_ok, upto(part_ok, g - 1))
                for b in range(NB):
                    post(v.tensor_scalar(gt[:, b], imp[:, b], tb[:, b:b + 1], None, ALU.is_gt))
                    post(v.tensor_scalar(eq[:, b], imp[:, b], tb[:, b:b + 1], None, ALU.is_equal))
                sync()
                for b in range(NB):
                    post(v.tensor_tensor_scan(cg[:, b], gt[:, b], zrow[:], 0.0, ALU.add, ALU.add))
                    post(v.tensor_tensor_scan(ce[:, b], eq[:, b], zrow[:], 0.0, ALU.add, ALU.add))
                sync()
                link(v.tensor_copy(tot[:, 0:NB], cg[:, :, H - 1]))
                v.tensor_copy(tot[:, NB:2 * NB], ce[:, :, H - 1]).then_inc(tot_ok, 1)

            def find_ranks(g):
                dve.wait_ge(off_ok, upto(off_ok, g))
                post(v.tensor_copy(off[:, 0:8], tr[0:H, OFFS:OFFS + 8]))
                v.tensor_scalar(off[:, 8:12], tr[0:H, TOTS:TOTS + 4], -1.0, float(K), ALU.mult, ALU.add).then_inc(small_rd, 1)
                dve.wait_ge(small_rd, upto(small_rd, g))
                for b in range(NB):
                    post(v.tensor_scalar(ce[:, b], ce[:, b], off[:, 4 + b:5 + b], off[:, 8 + b:9 + b], ALU.add, ALU.min))
                post(v.tensor_tensor(off[:, 12:16], off[:, 4:8], off[:, 8:12], ALU.min))
                sync()
                for b in range(NB):
                    post(v.scalar_tensor_tensor(cs[:, b, 0:H], cg[:, b], off[:, b:b + 1], ce[:, b], op0=ALU.add, op1=ALU.add))
                post(v.tensor_tensor(startend[:, 0:NB], off[:, 0:4], off[:, 12:16], ALU.add))
                sync()
                post(v.tensor_copy(startend[:, NB:2 * NB], cs[:, :, H - 1]))
                for b in range(NB):
                    post(v.tensor_scalar(hot_a[:, b], iota_k, startend[:, b:b + 1], None, ALU.is_ge))
                sync()
                for b in range(NB - 1):
                    post(v.scalar_tensor_tensor(hot[:, b], iota_k, startend[:, NB + b:NB + b + 1], hot_a[:, b],
                                                op0=ALU.is_lt, op1=ALU.mult))
                v.scalar_tensor_tensor(hot[:, NB - 1], iota_k, startend[:, 2 * NB - 1:2 * NB], hot_a[:, NB - 1],
                                       op0=ALU.is_lt, op1=ALU.mult).then_inc(hot_ok, 1)

            def find_rest(g):
                post(v.tensor_tensor(gt[:, :, 1:H], cs[:, :, 1:H], cs[:, :, 0:H - 1], ALU.subtract))
                post(v.tensor_tensor(gt[:, :, 0], cs[:, :, 0], startend[:, 0:NB], ALU.subtract))
                sync()
                v.scalar_tensor_tensor(im[:].rearrange("p b j -> p (b j)"), gt[:].rearrange("p b j -> p (b j)"), 0.5,
                                       imp[:].rearrange("p b j -> p (b j)"), op0=ALU.is_lt, op1=ALU.mult).then_inc(im_ok, 1)

            def find_index(g):
                dve.wait_ge(pick_ok, upto(pick_ok, g))
                for half in range(2):
                    for b in range(NB):
                        k = NB * half + b
                        post(v.tensor_scalar(jcol[:, k], sc[0:HALF, half, 112 * b:112 * b + H], slot_col[:, half:half + 1], None,
                                             ALU.is_le, ALU.add, accum_out=col[:, k:k + 1]))
                sync()
                for half in range(2):
                    ks = slice(NB * half, NB * half + NB)
                    rows = sc[0:HALF, half, 0:448].rearrange("p (b j) -> p b j", j=112)[:, :, 110]
                    post(v.scalar_tensor_tensor(pixf[:, 2, ks], rows, float(H), col[:, ks], op0=ALU.mult, op1=ALU.add))
                    post(v.scalar_tensor_tensor(pixf[:, 0, ks], col[:, ks], float(H), rows, op0=ALU.mult, op1=ALU.add))
                sync()
                post(v.scalar_tensor_tensor(pixf[:, 0], pixf[:, 0], float(NB), tab_base, op0=ALU.mult, op1=ALU.add))
                post(v.tensor_tensor(pixf[:, 1], pixf[:, 2], imp_base, ALU.add))
                sync()
                if g >= 2:
                    dve.wait_ge(scat, upto(scat, g - 2))
                v.tensor_copy(idx[:, g % 2], pixf[:]).then_inc(idx_ok, 1)

            def importance_sum(g, n):
                if n == 0:
                    dve.wait_ge(y7_in, upto(y7_in, g))
                b = slice(2 * n, 2 * n + 2)
                v.reduce_sum(yy[:, b], y7[:, b].rearrange("p b k j -> p b j k"), AX).then_inc(y_ok, 1)

            def importance(g, n):
                if n == 0:
                    dve.wait_ge(gelu_ok, upto(gelu_ok, g))
                b = slice(2 * n, 2 * n + 2)
                link(v.tensor_scalar(yy[:, b], ge[:, b], 1.0, None, ALU.add))
                v.reciprocal(ge[:, b], yy[:, b]).then_inc(imp_ok, 1)

            def embed(g):
                post(v.tensor_scalar(diag[:, 0:128], ident, mom[:, g, 0:1], None, ALU.mult))
                v.tensor_scalar(diag[:, 128:256], ident, mom[:, g, 2:3], None, ALU.mult).then_inc(diag_ok, 1)
                dve.wait_ge(tok_in, upto(tok_in, g))
                dve.wait_ge(rep_ok, upto(rep_ok, g))
                m = ms[0:HALF, 0:128].rearrange("p (b c) -> p b c", c=C)
                r = ms[0:HALF, 128:256].rearrange("p (b c) -> p b c", c=C)
                for half in range(2):
                    ks = slice(NB * half, NB * half + NB)
                    post(v.tensor_tensor(tok[:, ks], tok_x[:, g % 2, ks], m, ALU.subtract))
                sync()
                for half in range(2):
                    ks = slice(NB * half, NB * half + NB)
                    post(v.tensor_tensor(tok[:, ks], tok[:, ks], r, ALU.mult))
                sync()
                link(v.tensor_tensor(tok[:], tok[:], tok_imp[:].unsqueeze(2).to_broadcast([HALF, 8, C]), ALU.mult))
                v.tensor_tensor(tok[:], tok[:], tok_pos[:], ALU.add).then_inc(tok_ok, 1)
                dve.wait_ge(qkv_ok, upto(qkv_ok, g))
                for half in range(2):
                    last = v.tensor_tensor(vpad[:, half, :, 0:HD],
                                           ms[0:HALF, 128 * half:128 * half + 128].rearrange("p (h d) -> p h d", d=HD),
                                           rep[:, 0].rearrange("p b (h d) -> p (b h) d", d=HD), ALU.add)
                    if half == 0:
                        post(last)
                last.then_inc(v_cp, 1)

            def least_of(g, k):
                dve.wait_ge(s_ok, upto(s_ok, g, k))
                if k >= 2:
                    dve.wait_ge(e_ok, upto(e_ok, g, k - 2))
                elif g:
                    dve.wait_ge(e_ok, upto(e_ok, g - 1))
                v.tensor_reduce(least[:, k % 2], sc[0:HALF, k % 2, 0:2 * K].rearrange("p (h q) -> p h q", q=K),
                                AX, ALU.min).then_inc(least_ok, 1)

            def values(g, unit):
                b, half = unit // 2, unit % 2
                dve.wait_ge(ot_tr, upto(ot_tr, g, unit))
                o = ms[0:HALF, 256:512].rearrange("p (h d) -> p h d", d=32)
                link(v.reciprocal(rden[:].rearrange("p a h -> p (a h)"), o[:, :, HD]))
                v.tensor_tensor(o_tok[:, half, b].rearrange("p (h d) -> p h d", d=HD), o[:, :, 0:HD],
                                rden[:].rearrange("p a h -> p (a h)").unsqueeze(2).to_broadcast([HALF, NH, HD]),
                                ALU.mult).then_inc(o_ok, 1)

            halves = slice(0, NB), slice(NB, 2 * NB)

            def norm_first(y, bias, res_in, out_v):
                for half in range(2):
                    post(v.tensor_tensor(out_v[:, halves[half]], y[:, halves[half]], rep[:, bias], ALU.add))
                sync()
                link(v.tensor_tensor(out_v[:], out_v[:], res_in[:], ALU.add))
                link(v.reduce_sum(rs[:, 0, :], out_v[:], AX))
                link(v.tensor_scalar(rs[:, 0, :], rs[:, 0, :], 1.0 / C, None, ALU.mult))
                link(v.tensor_tensor(out_v[:], out_v[:], rs[:, 0, :].unsqueeze(2).to_broadcast([HALF, 8, C]), ALU.subtract))
                link(v.tensor_tensor(sq, out_v[:], out_v[:], ALU.mult))
                link(v.reduce_sum(rs[:, 3, :], sq, AX))
                return v.tensor_scalar(rs[:, 1, :], rs[:, 3, :], 1.0 / C, EPS, ALU.mult, ALU.add)

            def norm_last(gain, shift, out_v):
                link(v.tensor_tensor(out_v[:], out_v[:], rs[:, 2, :].unsqueeze(2).to_broadcast([HALF, 8, C]), ALU.mult))
                for half in range(2):
                    post(v.tensor_tensor(out_v[:, halves[half]], out_v[:, halves[half]], rep[:, gain], ALU.mult))
                sync()
                post(v.tensor_tensor(out_v[:, halves[0]], out_v[:, halves[0]], rep[:, shift], ALU.add))
                return v.tensor_tensor(out_v[:, halves[1]], out_v[:, halves[1]], rep[:, shift], ALU.add)

            def unit_back(g, u):
                dve.wait_ge(rt_tr, upto(rt_tr, g, u))
                dve.wait_ge(wgt_ok, upto(wgt_ok, g, u))
                if u >= 2:
                    dve.wait_ge(out_w[u % 2], upto(out_w[u % 2], g, u // 2 - 1))
                elif g:
                    dve.wait_ge(out_w[u % 2], upto(out_w[u % 2], g - 1))
                n = ROWS[u] * H
                v.scalar_tensor_tensor(res[:, u % 2, 0:n], tr[:, 0:n], mom[:, g, 0:1], wgt[:, 0:n],
                                       op0=ALU.subtract, op1=ALU.mult).then_inc(res_ok, 1)

            for w in (ms, w_conv, wq, wk, wv, wo, w1, w2, y7, vpad, zrow, cvr):
                post(v.memset(w[:], 0.0))
            post(v.memset(eps_col[:, 0:1], -0.5))
            post(v.memset(eps_col[:, 1:2], 1.0))
            sync()
            v.memset(vpad[:, :, :, HD:HD + 1], 1.0).then_inc(dve_set, 1)
            dve.wait_ge(ready, 16 * NL)
            for b in range(NB):
                q = slice(C * b, C * b + C)
                post(v.tensor_copy(w_conv[q, :, KS * b:KS * b + KS], w_small[q]))
            post(v.tensor_copy(blk[:], blk_f))
            post(v.tensor_copy(bones[:], bones_f))
            for b in range(NB):
                post(v.tensor_copy(cs[:, b, 110:111], row_col))
            link(v.tensor_scalar(bn[:, 7:8], bn[:, 4:5], EPS, None, ALU.add))
            link(v.tensor_scalar(bn[:, 6:7], bn[:, 0:1], bn[:, 3:4], None, ALU.subtract))
            v.memset(rs[:], 0.0).then_inc(dve_set, 1)
            dve.wait_ge(bn_rstd, upto(bn_rstd, 0))
            link(v.tensor_tensor(bn[:, 5:6], bn[:, 1:2], bn[:, 7:8], ALU.mult))
            link(v.tensor_scalar(bn[:, 6:7], bn[:, 6:7], bn[:, 5:6], bn[:, 2:3], ALU.mult, ALU.add))
            for s in SLOTS:
                for g, n in at(s, SEARCH, TOPK_STEPS):
                    count(g, n)
                for g, n in at(s, INTO, 14):
                    piece(g, 2 * n)
                for g, n in at(s, BACK, U):
                    unit_back(g, n)
                for g, n in at(s, SCORES, 16):
                    least_of(g, 2 * n)
                for g, n in at(s, INTO, 14):
                    piece(g, 2 * n + 1)
                for g, n in at(s, SEARCH, TOPK_STEPS):
                    refine(g, n)
                for g, n in at(s, SCORES, 16):
                    least_of(g, 2 * n + 1)
                for g, n in at(s, VALUES, 16):
                    if n % 2:
                        values(g, n // 2)
                for g, n in at(s, SUM, 2):
                    importance_sum(g, n)
                for g, n in at(s, GELU + 1, 2):
                    importance(g, n)
                for g, n in at(s, MASKS):
                    find_first(g)
                    find_masks(g)
                for g, n in at(s, RANKS):
                    find_ranks(g)
                for g, n in at(s, INDEX):
                    find_index(g)
                for g, n in at(s, REST):
                    find_rest(g)
                y = ms[0:HALF, 0:256].rearrange("p (k c) -> p k c", c=C)
                for g, n in at(s, MIX):
                    dve.wait_ge(wo_ok, upto(wo_ok, g))
                    norm_first(y, 1, tok, ra).then_inc(v1_ok, 1)
                for g, n in at(s, MIX + 1):
                    dve.wait_ge(r1_ok, upto(r1_ok, g))
                    norm_last(2, 3, ra).then_inc(t1_ok, 1)
                for g, n in at(s, FEED + 2):
                    dve.wait_ge(ff_ok, upto(ff_ok, g))
                    norm_first(y, 4, ra, rb).then_inc(v2_ok, 1)
                for g, n in at(s, FEED + 3):
                    dve.wait_ge(r2_ok, upto(r2_ok, g))
                    link(norm_last(5, 6, rb))
                    v.tensor_tensor(rb[:], rb[:], tok_x[:, g % 2], ALU.add).then_inc(t2_ok, 1)
                for g, n in at(s, INTO + 14):
                    moments(g)
                for g, n in at(s, EMBED):
                    embed(g)


def constants(H, C, NB, NH, K):
    import numpy as np

    def wide(a):
        a = np.asarray(a, np.float32)
        return np.concatenate([a, np.zeros((128 - a.shape[0], a.shape[1]), np.float32)])

    p = np.arange(128)
    rows = np.arange(H)
    c100 = np.arange(100)
    slots = np.arange(96)
    return np.concatenate([wide(a) for a in (
        np.eye(128), np.ones((128, 128)), rows[:, None] < rows[None, :], c100[:, None] // 25 == c100[None, :] // 25,
        (p[:, None] // (C // NH)) == np.arange(NB * NH)[None, :], np.tile(np.arange(K), (H, 1)),
        np.stack([slots, slots + 96], 1), rows[:, None], c100[:, None] == 25 * np.arange(NB)[None, :],
        np.tile(np.tile(np.arange(NB), 2), (96, 1)), np.tile(np.tile(np.arange(NB), 2) * H * H, (96, 1)),
        np.arange(12)[:, None] % NB == p[None, :] // C,
    )], axis=1).astype(np.float32)


def positions(seq_len, dim):
    import numpy as np
    pos = np.arange(seq_len, dtype=np.float32)[:, None]
    div = np.exp(np.arange(0, dim, 2, dtype=np.float32) * -(np.log(10000.0) / dim))
    pe = np.zeros((seq_len, dim), dtype=np.float32)
    pe[:, 0::2] = np.sin(pos * div)
    pe[:, 1::2] = np.cos(pos * div)
    return pe


def kernel(**inputs):
    import numpy as np
    import concourse.bacc as bacc
    from concourse import mybir
    from concourse.bass_utils import run_bass_kernel_spmd

    a = {k.removeprefix("L0_conv_"): np.asarray(v) for k, v in inputs.items()}
    B, C, H, _ = a["x"].shape
    arrays = {
        "in_x": a["x"],
        "in_conv_w": a["conv_w"][0].transpose(0, 2, 1),
        "in_conv_b": a["conv_b"], "in_bn_g": a["bn_g"], "in_bn_b": a["bn_b"], "in_bn_m": a["bn_m"], "in_bn_v": a["bn_v"],
        "in_w_qkvT": a["w_qkv"].T, "in_b_qkv": a["b_qkv"], "in_w_oT": a["w_o"].T, "in_b_o": a["b_o"],
        "in_ln1_g": a["ln1_g"], "in_ln1_b": a["ln1_b"], "in_w1T": a["w1"].T, "in_b1": a["b1"],
        "in_w2T": a["w2"].T, "in_b2": a["b2"], "in_ln2_g": a["ln2_g"], "in_ln2_b": a["ln2_b"],
        "in_pos": positions(H * H, C), "in_const": constants(H, C, 128 // C, 8, 192),
    }
    arrays = {k: np.ascontiguousarray(v) for k, v in arrays.items()}
    nc = bacc.Bacc("TRN2", target_bir_lowering=False, num_devices=1)
    args = [nc.dram_tensor(k, v.shape, mybir.dt.from_np(v.dtype), kind="ExternalInput").ap() for k, v in arrays.items()]
    out = nc.dram_tensor("out", a["x"].shape, mybir.dt.float32, kind="ExternalOutput").ap()
    preact_conv_token_attention(nc, *args, out)
    r = run_bass_kernel_spmd(nc, [arrays], core_ids=[0])
    return r.results[0]["out"]
```

```python
import concourse.bass as bass
from concourse import mybir
from contextlib import ExitStack


def preact_conv_token_attention(
    nc, x, conv_w, conv_b, bn_g, bn_b, bn_m, bn_v, w_qkvT, b_qkv, w_oT, b_o, ln1_g, ln1_b,
    w1T, b1, w2T, b2, ln2_g, ln2_b, pos, const, out,
):
    f32, bf16, fp16, u32 = mybir.dt.float32, mybir.dt.bfloat16, mybir.dt.float16, mybir.dt.uint32
    ALU, ACT, AX = mybir.AluOpType, mybir.ActivationFunctionType, mybir.AxisListType.X

    B, C, H, _ = x.shape
    HW = H * H
    NB = 128 // C
    G = B // NB
    NH, HD = 8, C // 8
    K, HALF = 192, 96
    KS, DIL = 7, 5
    U = 28
    ROWS = [4] * 27 + [2]
    TABLES = 7
    XC, XROWS = 5, H // 5
    FCH, FL = 25, HW // 25
    EPS = 1e-5
    TOPK_STEPS = 25

    table = [nc.dram_tensor(f"table{n}", [HW * NB, C], f32).ap() for n in range(TABLES)]
    table_jt = [t.rearrange("(j i b) c -> j i (b c)", j=H, b=NB) for t in table]
    conv_rows = nc.dram_tensor("conv_rows", [NB * KS, 7, 16, H], f32).ap()
    imp_flat = [nc.dram_tensor(f"imp_flat{n}", [NB * HW, 1], f32).ap() for n in range(2)]
    parts_dram = nc.dram_tensor("parts_dram", [G, 3, NB, H, H], bf16).ap()

    ctx = ExitStack()
    with ctx:
        def sb(name, shape, dt=f32):
            return ctx.enter_context(nc.sbuf_tensor(name, shape, dt))

        def pb(name, shape, dt=f32):
            return ctx.enter_context(nc.psum_tensor(name, shape, dt))

        counted = {}

        def raised(name, per=1, step=1):
            s = ctx.enter_context(nc.semaphore(name))
            counted[s.name] = per, step
            return s

        def upto(s, g, k=None):
            per, step = counted[s.name]
            return step * (per * g + (per if k is None else k + 1))

        NCONST = const.shape[1]
        cst = sb("cst", [128, NCONST])
        at = [0]

        def take(p, n):
            v = cst[0:p, at[0]:at[0] + n]
            at[0] += n
            return v

        ident = take(128, 128)
        ones = take(128, 128)
        tri = take(H, H)
        blk_f = take(100, 100)
        head_mask = take(128, NB * NH)
        iota_k = take(H, K)
        slot_col = take(HALF, 2)
        row_col = take(H, 1)
        first_chunk = take(100, NB)
        tab_base = take(HALF, 8)
        imp_base = take(HALF, 8)
        bones_f = take(12, 128)
        blk = sb("blk", [100, 100], fp16)
        bones = sb("bones", [12, 128], bf16)
        zrow = sb("zrow", [H, H])

        w_conv = sb("w_conv", [128, KS, 32])
        w_small = sb("w_small", [128, KS, KS])
        wq = sb("wq", [128, 128])
        wk = sb("wk", [128, 128])
        wv = sb("wv", [128, 128])
        wo = sb("wo", [128, 128])
        w1 = sb("w1", [128, 2, 128])
        w2 = sb("w2", [128, 64])
        qk_bias = sb("qk_bias", [128, 2])
        b1_col = sb("b1_col", [128, 1])
        rep = sb("rep", [HALF, 7, NB, C])
        bn = sb("bn", [H, 8])
        eps_col = sb("eps_col", [128, 2])

        X = [sb(f"X{p}", [128, H, H]) for p in range(2)]
        xt = sb("xt", [H, 2, 4, 128])
        rt = sb("rt", [H, 4, 4, 128])
        imp_b = sb("imp_b", [12, 4, 4 * H], bf16)
        wgt = sb("wgt", [128, 4 * H])
        res = sb("res", [128, 3, 4 * H])
        stats = sb("stats", [128, 25, 6])
        mom = sb("mom", [128, G, 6])
        cvr = sb("cvr", [128, 2, 4 * H])
        y7 = sb("y7", [H, NB, KS, H])
        yy = sb("yy", [H, NB, H])
        ge = sb("ge", [H, NB, H])
        imp = sb("imp", [H, NB, H])
        flat = sb("flat", [100, FL])
        th = sb("th", [100, 4])
        cnt = sb("cnt", [100, 1], fp16)
        tsel = sb("tsel", [100, NB])
        tb = sb("tb", [H, NB])
        gt = sb("gt", [H, NB, H], bf16)
        eq = sb("eq", [H, NB, H], bf16)
        cg = sb("cg", [H, NB, H], bf16)
        ce = sb("ce", [H, NB, H])
        tot = sb("tot", [H, 8])
        off = sb("off", [H, 16])
        startend = sb("startend", [H, 2 * NB])
        cs = sb("cs", [H, NB, 112], bf16)
        hot_a = sb("hot_a", [H, NB, K], bf16)
        hot = sb("hot", [H, NB, K], bf16)
        junk = hot_a[0:100].rearrange("p b k -> p (b k)")[:, 0:FL]
        im = ce
        parts = sb("parts", [H, 3, NB, H], bf16)
        jcol = yy[0:HALF].rearrange("p b j -> p (b j)").bitcast(bf16).rearrange("p (k j) -> p k j", j=H)
        col = sb("col", [HALF, 8])
        pixf = sb("pixf", [HALF, 3, 8])
        idx = sb("idx", [HALF, 2, 3, 8], u32)
        tok_x = sb("tok_x", [HALF, 2, 8, C])
        tok_pos = sb("tok_pos", [HALF, 8, C])
        tok_imp = sb("tok_imp", [HALF, 8])
        diag = sb("diag", [128, 256])
        tok = sb("tok", [HALF, 8, C])
        tok_t = sb("tok_t", [128, K])
        q_t = sb("q_t", [128, K])
        k_t = sb("k_t", [128, K])
        vpad = sb("vpad", [HALF, 2, NB * NH, 8])
        qm = sb("qm", [128, NH, K])
        pr = sb("pr", [HALF, 2, NH, K])
        least = sb("least", [HALF, 2, 2])
        pt = sb("pt", [HALF, 2, 2, NH, HALF])
        o_t = sb("o_t", [128, 2, HALF])
        rden = sb("rden", [HALF, 2, 4])
        o_tok = sb("o_tok", [HALF, 2, NB, C])
        act_t = q_t
        hid = qm[:, 0:2]
        sq = diag[0:HALF].rearrange("p (k c) -> p k c", c=C)
        ra = sb("ra", [HALF, 8, C])
        rb = sb("rb", [HALF, 8, C])
        rs = sb("rs", [HALF, 4, 8])

        cv = pb("cv", [128, 512])
        xb = pb("xb", [128, 512])
        tr = pb("tr", [128, 512])
        ib = pb("ib", [128, 512])
        sc = pb("sc", [128, 2, 512])
        pp = pb("pp", [128, 512])
        ms = pb("ms", [128, 512])
        COUNT, OFFS, TOTS, THR = 440, 468, 476, 484

        cst_in = raised("cst_in", 1, 16)
        ready = raised("ready", 1, 16)
        dve_set = raised("dve_set", 2)
        bn_rstd = raised("bn_rstd")
        x_in = [[raised(f"x_in{p}_{c}", 1, 16) for c in range(XC)] for p in range(2)]
        xt_tr = raised("xt_tr", U)
        xt_cp = raised("xt_cp", U)
        tab_first = [raised(f"tab_first{i}", U // 4, 16) for i in range(4)]
        tab_w = [raised(f"tab_w{i}", U // 2, 16) for i in range(2)]
        var_ok = raised("var_ok")
        rstd_ok = raised("rstd_ok")
        xn_ok = raised("xn_ok", XC)
        conv_ok = raised("conv_ok", 7)
        cv_cp = raised("cv_cp", 7)
        cv_w = [raised(f"cv_w{i}", [4, 3][i], 64) for i in range(2)]
        y7_in = raised("y7_in", 1, 16 * KS)
        y_ok = raised("y_ok", 2)
        gelu_ok = raised("gelu_ok")
        imp_ok = raised("imp_ok", 2)
        imp_w = raised("imp_w", 1, 16)
        flat_in = raised("flat_in", 1, 16)
        imp_in = raised("imp_in", 1, 16)
        cnt_ok = raised("cnt_ok", TOPK_STEPS)
        cnt_sum = raised("cnt_sum", TOPK_STEPS)
        small_rd = raised("small_rd", TOPK_STEPS + 2)
        tsel_ok = raised("tsel_ok")
        tb_ok = raised("tb_ok")
        tot_ok = raised("tot_ok")
        off_ok = raised("off_ok")
        hot_ok = raised("hot_ok")
        pick_ok = raised("pick_ok")
        im_ok = raised("im_ok")
        part_ok = raised("part_ok")
        parts_w = raised("parts_w", 1, 16)
        idx_ok = raised("idx_ok")
        tok_in = raised("tok_in", 1, 24 * 16)
        diag_ok = raised("diag_ok")
        rep_ok = raised("rep_ok")
        tok_ok = raised("tok_ok")
        tokt_ok = raised("tokt_ok")
        tokt_cp = raised("tokt_cp")
        qkv_ok = raised("qkv_ok")
        qk_cp = raised("qk_cp", 2)
        v_cp = raised("v_cp")
        qm_ok = raised("qm_ok", 4 * NB)
        s_ok = raised("s_ok", 32)
        least_ok = raised("least_ok", 32)
        e_ok = raised("e_ok", 32)
        pt_tr = raised("pt_tr", 32)
        pt_cp = raised("pt_cp", 32)
        pv_ok = raised("pv_ok", 8)
        ot_cp = raised("ot_cp", 8)
        ot_tr = raised("ot_tr", 8)
        o_ok = raised("o_ok", 8)
        oa_tr = raised("oa_tr")
        oa_cp = raised("oa_cp")
        wo_ok = raised("wo_ok")
        v1_ok = raised("v1_ok")
        r1_ok = raised("r1_ok")
        t1_ok = raised("t1_ok")
        t1_tr = raised("t1_tr")
        t1_cp = raised("t1_cp")
        h_ok = raised("h_ok")
        h_cp = raised("h_cp")
        ff_ok = raised("ff_ok")
        v2_ok = raised("v2_ok")
        r2_ok = raised("r2_ok")
        t2_ok = raised("t2_ok")
        scat = raised("scat", 1, 8 * 16)
        rt_in = [raised(f"rt_in{i}", U // 4, 16) for i in range(4)]
        ib_in = [raised(f"ib_in{i}", U // 4, 16) for i in range(4)]
        rt_tr = raised("rt_tr", U)
        ib_ok = raised("ib_ok", U)
        wgt_ok = raised("wgt_ok", U)
        res_ok = raised("res_ok", U)
        fin_ok = raised("fin_ok", U)
        out_w = [raised(f"out_w{i}", None, 16) for i in range(3)]
        own = {e: ctx.enter_context(nc.semaphore(f"own_{e}")) for e in ("dve", "act", "pool")}

        block = ctx.enter_context(nc.Block())

        LOAD, INTO, NORMAL = (-48, -44, -36, -32, -28), -34, (-5, 2, 5, 8, 12)
        TAPS, SUM, GELU, IMP_OUT, FLAT = 29, 31, 33, 37, 38
        SEARCH, IMP_IN, MASKS, RANKS, PICK, INDEX = 40, 60, 65, 66, 68, 69
        GATHER, REST, SPLIT, PARTS_OUT = 70, 72, (78, 85, 86), 87
        EMBED, SCORES, TURN, VALUES = 77, 81, 83, 85
        MIX, SCATTER, BACK = 102, 109, 118
        SLOTS = range(LOAD[0], U * G + BACK)

        TWO_BANKS = next(g for g in range(G + 1) if U * g + BACK > U * (G - 1) + INTO + U - 1)

        def back_bank(g, u):
            return xb if g >= TWO_BANKS and u % 2 else tr

        def at(slot, first, n=1):
            g, k = (slot - first) // U, (slot - first) % U
            return [(g, k)] if k < n and 0 <= g < G else []

        loads = [0]

        @block.sync
        def _(sp):
            def load(dst, src):
                sp.dma_start(dst, src).then_inc(ready, 16)
                loads[0] += 1

            def load_x(g, c):
                if g >= 2:
                    sp.wait_ge(conv_ok, upto(conv_ok, g - 2, (XROWS * c + XROWS - 1) // 16))
                xs = x.rearrange("(g b) c h w -> g (b c) h w", b=NB)[g]
                r = slice(c * XROWS, (c + 1) * XROWS)
                sp.dma_start(X[g % 2][:, r, :], xs[:, r, :]).then_inc(x_in[g % 2][c], 16)

            sp.dma_start(cst[:], const).then_inc(cst_in, 16)
            for c in range(XC):
                load_x(0, c)
            for b in range(NB):
                load(w_small[C * b:C * b + C], conv_w)
            sp.wait_ge(dve_set, upto(dve_set, 0, 0))
            for b in range(NB):
                q = slice(C * b, C * b + C)
                for n, w in enumerate((wq, wk, wv)):
                    load(w[q, q], w_qkvT[:, n * C:(n + 1) * C])
                load(wo[q, q], w_oT)
                load(w1[q, b // 2, 64 * (b % 2):64 * (b % 2) + 64], w1T)
                for n in range(2):
                    load(qk_bias[q, n:n + 1], b_qkv[n * C:(n + 1) * C].rearrange("(c o) -> c o", o=1))
            for b in range(2):
                load(w2[64 * b:64 * b + 64, C * b:C * b + C], w2T)
                load(b1_col[64 * b:64 * b + 64, :], b1.rearrange("(c o) -> c o", o=1))
            for n, v in enumerate((b_qkv[2 * C:3 * C], b_o, ln1_g, ln1_b, b2, ln2_g, ln2_b)):
                load(rep[:, n], v.rearrange("(o p c) -> o p c", o=1, p=1).broadcast_to([HALF, NB, C]))
            for n, v in enumerate((conv_b, bn_g, bn_b, bn_m, bn_v)):
                load(bn[:, n:n + 1], v.rearrange("(o c) -> o c", o=1).broadcast_to([H, 1]))
            for c in range(XC):
                load_x(1, c)

            def table_out(g, u):
                if u == 0 and g >= TABLES:
                    for i in range(4):
                        sp.wait_ge(rt_in[i], upto(rt_in[i], g - TABLES))
                sp.wait_ge(xt_cp, upto(xt_cp, g, u))
                sp.dma_start(table_jt[g % TABLES][:, 4 * u:4 * u + ROWS[u], :], xt[:, u % 2, 0:ROWS[u], :]).then_inc(tab_w[u % 2], 16)

            def back_in(g, u):
                if u == 0:
                    sp.wait_ge(scat, upto(scat, g))
                    sp.wait_ge(parts_w, upto(parts_w, g))
                if u >= 4:
                    sp.wait_ge(rt_tr, upto(rt_tr, g, u - 4))
                    sp.wait_ge(ib_ok, upto(ib_ok, g, u - 4))
                elif g >= 1:
                    sp.wait_ge(rt_tr, upto(rt_tr, g - 1, U - 4 + u))
                    sp.wait_ge(ib_ok, upto(ib_ok, g - 1, U - 4 + u))
                nr = ROWS[u]
                sp.dma_start(rt[:, u % 4, 0:nr, :], table_jt[g % TABLES][:, 4 * u:4 * u + nr, :]).then_inc(rt_in[u % 4], 16)
                sp.dma_start(imp_b[:, u % 4, 0:nr * H],
                             parts_dram[g, :, :, 4 * u:4 * u + nr, :].rearrange("q b i j -> (q b) (i j)")
                             ).then_inc(ib_in[u % 4], 16)

            def out_store(g, u):
                sp.wait_ge(fin_ok, upto(fin_ok, g, u))
                og = out.rearrange("(g b) c h w -> g (b c) h w", b=NB)[g]
                nr = ROWS[u]
                sp.dma_start(og[:, 4 * u:4 * u + nr, :].rearrange("p i j -> p (i j)"),
                             res[:, (U * g + u) % 3, 0:nr * H]).then_inc(out_w[(U * g + u) % 3], 16)

            def round_out(g, t):
                sp.wait_ge(cv_cp, upto(cv_cp, g, t))
                if t == 0 and g:
                    sp.wait_ge(y7_in, upto(y7_in, g - 1))
                for q in range(4):
                    sp.dma_start(conv_rows[:, t, 4 * q:4 * q + 4, :].rearrange("p r j -> p (r j)"),
                                 cvr[32 * q:32 * q + NB * KS, t % 2, :]).then_inc(cv_w[t % 2], 16)

            def taps_in(g):
                for i in range(2):
                    sp.wait_ge(cv_w[i], upto(cv_w[i], g))
                if g:
                    sp.wait_ge(y_ok, upto(y_ok, g - 1))
                rows = conv_rows.rearrange("(b k) t r j -> k (t r) b j", k=KS)
                for ki in range(KS):
                    o = DIL * (ki - 3)
                    i0, i1 = max(0, -o), min(H, H - o)
                    sp.dma_start(y7[i0:i1, :, ki, :], rows[ki, i0 + o:i1 + o, :, :]).then_inc(y7_in, 16)

            def imp_out(g):
                sp.wait_ge(imp_ok, upto(imp_ok, g))
                if g >= 2:
                    sp.wait_ge(tok_in, upto(tok_in, g - 2))
                    sp.wait_ge(imp_in, upto(imp_in, g - 2))
                sp.dma_start(imp_flat[g % 2].rearrange("(b i j) o -> i b (j o)", b=NB, i=H), ge[:]).then_inc(imp_w, 16)

            def flat_load(g):
                sp.wait_ge(imp_w, upto(imp_w, g))
                if g:
                    sp.wait_ge(cnt_ok, upto(cnt_ok, g - 1))
                sp.dma_start(flat[:], imp_flat[g % 2].rearrange("(p f) o -> p (f o)", f=FL)).then_inc(flat_in, 16)

            def imp_load(g):
                if g:
                    sp.wait_ge(im_ok, upto(im_ok, g - 1))
                sp.dma_start(imp[:], imp_flat[g % 2].rearrange("(b i j) o -> i b (j o)", b=NB, i=H)).then_inc(imp_in, 16)

            def parts_out(g):
                sp.wait_ge(part_ok, upto(part_ok, g))
                sp.dma_start(parts_dram[g].rearrange("q b i j -> i (q b) j"),
                             parts[:].rearrange("p q b j -> p (q b) j")).then_inc(parts_w, 16)

            for s in SLOTS:
                for c in range(XC):
                    for g, n in at(s, LOAD[c]):
                        if g >= 2:
                            load_x(g, c)
                for g, n in at(s, INTO, U):
                    if g:
                        table_out(g, n)
                for g, n in at(s, 3, 25):
                    if n % 4 == 0:
                        round_out(g, n // 4)
                for g, n in at(s, BACK - 2):
                    for u in range(4):
                        back_in(g, u)
                for g, n in at(s, BACK + 1, U - 4):
                    back_in(g, n + 4)
                for g, n in at(s, BACK, U):
                    out_store(g, n)
                for g, n in at(s, TAPS):
                    taps_in(g)
                for g, n in at(s, IMP_OUT):
                    imp_out(g)
                for g, n in at(s, FLAT):
                    flat_load(g)
                for g, n in at(s, IMP_IN):
                    imp_load(g)
                for g, n in at(s, PARTS_OUT):
                    parts_out(g)
            for n in range(U * G - 3, U * G):
                sp.wait_ge(out_w[n % 3], 16 * (n // 3 + 1))

        NL = loads[0]

        @block.tensor
        def _(pe):
            mm = nc.tensor.matmul

            def unit_in(g, u):
                for c in range(XC):
                    if 4 * (u - 1) + 3 < c * XROWS <= 4 * u + ROWS[u] - 1:
                        pe.wait_ge(x_in[g % 2][c], upto(x_in[g % 2][c], g // 2))
                if g == 0 and u >= 2:
                    pe.wait_ge(xt_cp, upto(xt_cp, g, u - 2))
                elif g and u:
                    pe.wait_ge(xt_cp, upto(xt_cp, g, u - 1))
                elif g:
                    pe.wait_ge(xt_cp, upto(xt_cp, g - 1))
                bank = tr if g == 0 and u % 2 else xb
                for r in range(ROWS[u]):
                    last = nc.tensor.transpose(bank[0:H, 128 * r:128 * r + 128], X[g % 2][:, 4 * u + r, :], ident)
                last.then_inc(xt_tr, 1)

            def conv_part(g, n, first, last_m):
                t, part = n // 4, n % 4
                for c in range(XC):
                    if part == 0 and first == 0 and 16 * t - 1 < c * XROWS <= 16 * t + 15:
                        pe.wait_ge(xn_ok, upto(xn_ok, g, c))
                if part == 0 and first == 0:
                    if t:
                        pe.wait_ge(cv_cp, upto(cv_cp, g, t - 1))
                    elif g:
                        pe.wait_ge(cv_cp, upto(cv_cp, g - 1))
                order = [3, 0, 1, 2, 4, 5, 6]
                for m in range(7 * part + first, 7 * part + last_m):
                    kj, q = order[m // 4], m % 4
                    u = 4 * t + q
                    shift, nr = DIL * (kj - 3), ROWS[u]
                    j0, j1 = max(0, -shift), min(H, H - shift)
                    o = cv[32 * q:32 * q + 32, 0:nr * H].rearrange("p (r j) -> p r j", j=H)
                    last = mm(o[:, :, j0:j1], w_conv[:, kj, :], X[g % 2][:, 4 * u:4 * u + nr, j0 + shift:j1 + shift],
                              start=m < 4, stop=m >= 24, skip_group_check=True)
                if part == 3 and last_m == 7:
                    last.then_inc(conv_ok, 1)

            searched, backed, backed_xb = [], [], []

            def count(g, k):
                for value in backed[-1:]:
                    pe.wait_ge(res_ok, value)
                pe.wait_ge(cnt_ok, upto(cnt_ok, g, k))
                mm(tr[0:100, COUNT + k:COUNT + k + 1], blk[:], cnt[:], start=True, stop=True).then_inc(cnt_sum, 1)
                searched.append(upto(small_rd, g, k))

            def unit_back(g, u):
                nr = ROWS[u]
                bank = back_bank(g, u)
                if bank is tr:
                    for value in backed[-1:]:
                        pe.wait_ge(res_ok, value)
                    for value in searched[-1:]:
                        pe.wait_ge(small_rd, value)
                    backed.append(upto(res_ok, g, u))
                else:
                    pe.wait_ge(xt_cp, upto(xt_cp, G - 1))
                    for value in backed_xb[-1:]:
                        pe.wait_ge(res_ok, value)
                    backed_xb.append(upto(res_ok, g, u))
                pe.wait_ge(rt_in[u % 4], upto(rt_in[u % 4], g, u // 4))
                for r in range(nr):
                    last = nc.tensor.transpose(bank[:, H * r:H * r + H], rt[:, u % 4, r, :], ident[0:H, 0:H])
                last.then_inc(rt_tr, 1)

            def spread(g, u):
                nr = ROWS[u]
                pe.wait_ge(ib_in[u % 4], upto(ib_in[u % 4], g, u // 4))
                if u:
                    pe.wait_ge(wgt_ok, upto(wgt_ok, g, u - 1))
                elif g:
                    pe.wait_ge(wgt_ok, upto(wgt_ok, g - 1))
                mm(ib[:, 0:nr * H], bones[:], imp_b[:, u % 4, 0:nr * H], start=True, stop=True).then_inc(ib_ok, 1)

            def thresholds(g):
                for value in backed[-1:]:
                    pe.wait_ge(res_ok, value)
                searched.append(upto(small_rd, g, TOPK_STEPS))
                pe.wait_ge(tsel_ok, upto(tsel_ok, g))
                mm(tr[0:H, THR:THR + NB], ones[0:100, 0:H], tsel[:], start=True, stop=True).then_inc(tb_ok, 1)

            def offsets(g):
                for value in backed[-1:]:
                    pe.wait_ge(res_ok, value)
                searched.append(upto(small_rd, g))
                pe.wait_ge(tot_ok, upto(tot_ok, g))
                mm(tr[0:H, OFFS:OFFS + 8], tri, tot[:], start=True, stop=True)
                mm(tr[0:H, TOTS:TOTS + 8], ones[0:H, 0:H], tot[:], start=True, stop=True).then_inc(off_ok, 1)

            def pick(g):
                pe.wait_ge(hot_ok, upto(hot_ok, g))
                if g >= 1:
                    pe.wait_ge(e_ok, upto(e_ok, g - 1))
                for half in range(2):
                    for b in range(NB):
                        last = mm(sc[0:HALF, half, 112 * b:112 * b + 111], hot[:, b, HALF * half:HALF * half + HALF],
                                  cs[:, b, 0:111], start=True, stop=True)
                last.then_inc(pick_ok, 1)

            def moments_spread(g):
                pe.wait_ge(diag_ok, upto(diag_ok, g))
                mm(pp[0:HALF, 0:256], ones[:, 0:HALF], diag[:], start=True, stop=True).then_inc(rep_ok, 1)

            def tokens_turn(g):
                pe.wait_ge(tok_ok, upto(tok_ok, g))
                for half in range(2):
                    last = nc.tensor.transpose(pp[:, HALF * half:HALF * half + HALF],
                                               tok[:, NB * half:NB * half + NB, :].rearrange("p b c -> p (b c)"), ident[0:HALF, 0:HALF])
                last.then_inc(tokt_ok, 1)

            def project(g):
                pe.wait_ge(tokt_cp, upto(tokt_cp, g))
                if g:
                    pe.wait_ge(v2_ok, upto(v2_ok, g - 1))
                mm(sc[:, 0, 0:K], wq[:], tok_t[:], start=True, stop=True)
                mm(sc[:, 1, 0:K], wk[:], tok_t[:], start=True, stop=True)
                for half in range(2):
                    last = mm(ms[0:HALF, 128 * half:128 * half + 128], tok_t[:, HALF * half:HALF * half + HALF], wv[:],
                              start=True, stop=True)
                last.then_inc(qkv_ok, 1)

            def scores(g, k):
                b, half, pair = k // 8, (k // 4) % 2, k % 4
                if k == 0:
                    pe.wait_ge(qk_cp, upto(qk_cp, g))
                if half == 0:
                    pe.wait_ge(qm_ok, upto(qm_ok, g, 4 * b + pair))
                if k >= 2:
                    pe.wait_ge(e_ok, upto(e_ok, g, k - 2))
                for h in range(2):
                    last = mm(sc[0:HALF, k % 2, K * h:K * h + K], qm[:, 2 * pair + h, HALF * half:HALF * half + HALF],
                              k_t[:], start=True, stop=True)
                last.then_inc(s_ok, 1)

            def turn(g, k):
                unit, kh, hg = k // 4, (k // 2) % 2, k % 2
                if k % 4 == 0:
                    pe.wait_ge(e_ok, upto(e_ok, g, 4 * unit + 3))
                if k:
                    pe.wait_ge(pt_cp, upto(pt_cp, g, k - 1))
                for h in range(4):
                    last = nc.tensor.transpose(pp[0:HALF, HALF * h:HALF * h + HALF],
                                               pr[:, unit % 2, 4 * hg + h, HALF * kh:HALF * kh + HALF], ident[0:HALF, 0:HALF])
                last.then_inc(pt_tr, 1)

            def values(g, unit):
                b = unit // 2
                if unit == 0:
                    pe.wait_ge(v_cp, upto(v_cp, g))
                else:
                    pe.wait_ge(o_ok, upto(o_ok, g, unit - 1))
                pe.wait_ge(pt_cp, upto(pt_cp, g, 4 * unit + 3))
                for hh in range(2):
                    for kh in range(2):
                        for q in range(4):
                            h = 4 * hh + q
                            last = mm(ms[32 * q:32 * q + 8, HALF * hh:HALF * hh + HALF], vpad[:, kh, NH * b + h, :],
                                      pt[:, unit % 2, kh, h, :], start=kh == 0, stop=kh == 1, skip_group_check=True)
                last.then_inc(pv_ok, 1)

            def values_turn(g, unit):
                pe.wait_ge(ot_cp, upto(ot_cp, g, unit))
                for hh in range(2):
                    last = nc.tensor.transpose(ms[0:HALF, 256 + 128 * hh:384 + 128 * hh], o_t[:, hh, :], ident)
                last.then_inc(ot_tr, 1)

            def mix(g):
                pe.wait_ge(o_ok, upto(o_ok, g))
                for half in range(2):
                    last = nc.tensor.transpose(pp[:, HALF * half:HALF * half + HALF],
                                               o_tok[:, half].rearrange("p b c -> p (b c)"), ident[0:HALF, 0:HALF])
                last.then_inc(oa_tr, 1)

            def mix_out(g):
                pe.wait_ge(oa_cp, upto(oa_cp, g))
                for half in range(2):
                    last = mm(ms[0:HALF, 128 * half:128 * half + 128], act_t[:, HALF * half:HALF * half + HALF], wo[:],
                              start=True, stop=True)
                last.then_inc(wo_ok, 1)

            def feed(g):
                pe.wait_ge(t1_ok, upto(t1_ok, g))
                for half in range(2):
                    last = nc.tensor.transpose(pp[:, HALF * half:HALF * half + HALF],
                                               ra[:, NB * half:NB * half + NB, :].rearrange("p b c -> p (b c)"), ident[0:HALF, 0:HALF])
                last.then_inc(t1_tr, 1)

            def feed_in(g):
                pe.wait_ge(t1_cp, upto(t1_cp, g))
                for pair in range(2):
                    last = mm(sc[:, 0, K * pair:K * pair + K], w1[:, pair, :], act_t[:], start=True, stop=True)
                last.then_inc(h_ok, 1)

            def feed_last(g):
                pe.wait_ge(h_cp, upto(h_cp, g))
                for half in range(2):
                    for pair in range(2):
                        last = mm(ms[0:HALF, 128 * half + 64 * pair:128 * half + 64 * pair + 64],
                                  hid[:, pair, HALF * half:HALF * half + HALF], w2[:], start=True, stop=True)
                last.then_inc(ff_ok, 1)

            pe.wait_ge(cst_in, upto(cst_in, 0))
            for s in SLOTS:
                if s == 0:
                    pe.wait_ge(ready, 16 * NL)
                    pe.wait_ge(dve_set, upto(dve_set, 0))
                for g, n in at(s, INTO, U):
                    unit_in(g, n)
                for g, n in at(s, BACK, U):
                    unit_back(g, n)
                for g, n in at(s, SCORES, 16):
                    scores(g, 2 * n)
                for g, n in at(s, 0, U):
                    conv_part(g, n, 0, 4)
                for g, n in at(s, TURN, 16):
                    turn(g, 2 * n)
                for g, n in at(s, BACK - 1, U):
                    spread(g, n)
                for g, n in at(s, MASKS):
                    thresholds(g)
                for g, n in at(s, RANKS):
                    offsets(g)
                for g, n in at(s, MIX + 1):
                    mix_out(g)
                for g, n in at(s, MIX + 3):
                    feed(g)
                for g, n in at(s, MIX + 4):
                    feed_in(g)
                for g, n in at(s, MIX + 5):
                    feed_last(g)
                for g, n in at(s, EMBED + 1):
                    moments_spread(g)
                for g, n in at(s, EMBED + 2):
                    tokens_turn(g)
                for g, n in at(s, EMBED + 3):
                    project(g)
                for g, n in at(s, SCORES, 16):
                    scores(g, 2 * n + 1)
                for g, n in at(s, SEARCH, TOPK_STEPS):
                    count(g, n)
                for g, n in at(s, 0, U):
                    conv_part(g, n, 4, 7)
                for g, n in at(s, TURN, 16):
                    turn(g, 2 * n + 1)
                for g, n in at(s, VALUES, 16):
                    (values_turn if n % 2 else values)(g, n // 2)
                for g, n in at(s, PICK):
                    pick(g)
                for g, n in at(s, MIX):
                    mix(g)

        @block.scalar
        def _(act):
            mine = [0]
            A = nc.scalar.activation

            def link(ins):
                mine[0] += 1
                ins.then_inc(own["act"], 1)
                act.wait_ge(own["act"], mine[0])

            def unit_in(g, u):
                act.wait_ge(xt_tr, upto(xt_tr, g, u))
                nr = ROWS[u]
                if g == 0:
                    if u >= 4:
                        act.wait_ge(tab_first[u % 4], upto(tab_first[u % 4], 0, u // 4 - 1))
                    bank = tr if u % 2 else xb
                    nc.scalar.copy(rt[:, u % 4, 0:nr, :].rearrange("p r c -> p (r c)"), bank[0:H, 0:128 * nr]).then_inc(xt_cp, 1)
                    act.wait_ge(xt_cp, upto(xt_cp, g, u))
                    act.dma_start(table_jt[g][:, 4 * u:4 * u + nr, :], rt[:, u % 4, 0:nr, :]).then_inc(tab_first[u % 4], 16)
                    return
                if u >= 2:
                    act.wait_ge(tab_w[u % 2], upto(tab_w[u % 2], g - 1, u // 2 - 1))
                elif g >= 2:
                    act.wait_ge(tab_w[u % 2], upto(tab_w[u % 2], g - 2))
                nc.scalar.copy(xt[:, u % 2, 0:nr, :].rearrange("p r c -> p (r c)"), xb[0:H, 0:128 * nr]).then_inc(xt_cp, 1)

            def round_copy(g, t):
                act.wait_ge(conv_ok, upto(conv_ok, g, t))
                if t >= 2:
                    act.wait_ge(cv_w[t % 2], upto(cv_w[t % 2], g, t // 2 - 1))
                elif g:
                    act.wait_ge(cv_w[t % 2], upto(cv_w[t % 2], g - 1))
                if t < 6:
                    nc.scalar.copy(cvr[:, t % 2, :], cv[:, 0:4 * H]).then_inc(cv_cp, 1)
                else:
                    link(nc.scalar.copy(cvr[96:128, 0, 0:2 * H], cv[96:128, 0:2 * H]))
                    nc.scalar.copy(cvr[0:96, 0, :], cv[0:96, 0:4 * H]).then_inc(cv_cp, 1)

            def importance(g):
                act.wait_ge(y_ok, upto(y_ok, g))
                link(A(ge[:].rearrange("p b j -> p (b j)"), yy[:].rearrange("p b j -> p (b j)"), ACT.Gelu,
                       scale=bn[:, 5:6], bias=bn[:, 6:7]))
                A(ge[:], ge[:], ACT.Exp, scale=-1.0).then_inc(gelu_ok, 1)

            def unit_back(g, u):
                act.wait_ge(ib_ok, upto(ib_ok, g, u))
                if u:
                    act.wait_ge(res_ok, upto(res_ok, g, u - 1))
                elif g:
                    act.wait_ge(res_ok, upto(res_ok, g - 1))
                A(wgt[:, 0:ROWS[u] * H], ib[:, 0:ROWS[u] * H], ACT.Identity, scale=mom[:, g, 2:3],
                  bias=eps_col[:, 1:2]).then_inc(wgt_ok, 1)

            def embed(g):
                act.wait_ge(tokt_ok, upto(tokt_ok, g))
                nc.scalar.copy(tok_t[:], pp[:, 0:K]).then_inc(tokt_cp, 1)

            def project(g):
                act.wait_ge(qkv_ok, upto(qkv_ok, g))
                if g:
                    act.wait_ge(qm_ok, upto(qm_ok, g - 1))
                    act.wait_ge(s_ok, upto(s_ok, g - 1))
                A(q_t[:], sc[:, 0, 0:K], ACT.Identity, scale=-HD ** -0.5, bias=qk_bias[:, 0:1]).then_inc(qk_cp, 1)
                A(k_t[:], sc[:, 1, 0:K], ACT.Identity, bias=qk_bias[:, 1:2]).then_inc(qk_cp, 1)

            def exps(g, k):
                unit, pair = k // 4, k % 4
                act.wait_ge(least_ok, upto(least_ok, g, k))
                if pair == 0 and unit >= 2:
                    act.wait_ge(pt_tr, upto(pt_tr, g, 4 * (unit - 2) + 3))
                elif pair == 0 and g:
                    act.wait_ge(pt_tr, upto(pt_tr, g - 1))
                for h in range(2):
                    last = A(pr[:, unit % 2, 2 * pair + h, :], sc[0:HALF, k % 2, K * h:K * h + K], ACT.Exp,
                             scale=-1.0, bias=least[:, k % 2, h:h + 1])
                last.then_inc(e_ok, 1)

            def turn(g, k):
                unit, kh, hg = k // 4, (k // 2) % 2, k % 2
                act.wait_ge(pt_tr, upto(pt_tr, g, k))
                if k % 4 == 0 and unit >= 2:
                    act.wait_ge(pv_ok, upto(pv_ok, g, unit - 2))
                elif k % 4 == 0 and g:
                    act.wait_ge(pv_ok, upto(pv_ok, g - 1))
                nc.scalar.copy(pt[:, unit % 2, kh, 4 * hg:4 * hg + 4, :],
                               pp[0:HALF, 0:4 * HALF].rearrange("p (h q) -> p h q", q=HALF)).then_inc(pt_cp, 1)

            def values(g, unit):
                act.wait_ge(pv_ok, upto(pv_ok, g, unit))
                if unit:
                    act.wait_ge(ot_tr, upto(ot_tr, g, unit - 1))
                elif g:
                    act.wait_ge(ot_tr, upto(ot_tr, g - 1))
                nc.scalar.copy(o_t[:], ms[:, 0:2 * HALF].rearrange("p (a q) -> p a q", a=2)).then_inc(ot_cp, 1)

            def mix(g):
                act.wait_ge(oa_tr, upto(oa_tr, g))
                nc.scalar.copy(act_t[:], pp[:, 0:K]).then_inc(oa_cp, 1)

            def feed(g):
                act.wait_ge(t1_tr, upto(t1_tr, g))
                nc.scalar.copy(act_t[:], pp[:, 0:K]).then_inc(t1_cp, 1)

            def feed_in(g):
                act.wait_ge(h_ok, upto(h_ok, g))
                A(hid.rearrange("p a q -> p (a q)"), sc[:, 0, 0:2 * K], ACT.Relu, bias=b1_col[:]).then_inc(h_cp, 1)

            for s in SLOTS:
                if s == 0:
                    act.wait_ge(ready, 16 * NL)
                    act.wait_ge(dve_set, upto(dve_set, 0))
                    link(nc.scalar.mul(qk_bias[:, 0:1], qk_bias[:, 0:1], -HD ** -0.5))
                for g, n in at(s, INTO, U):
                    unit_in(g, n)
                for g, n in at(s, SCORES, 16):
                    exps(g, 2 * n)
                for g, n in at(s, TURN, 16):
                    turn(g, 2 * n)
                for g, n in at(s, BACK - 1, U):
                    unit_back(g, n)
                for g, n in at(s, SCORES, 16):
                    exps(g, 2 * n + 1)
                for g, n in at(s, TURN, 16):
                    turn(g, 2 * n + 1)
                for g, n in at(s, VALUES, 16):
                    if n % 2 == 0:
                        values(g, n // 2)
                for g, n in at(s, 0, U):
                    if n % 4 == 3:
                        round_copy(g, n // 4)
                for g, n in at(s, MIX):
                    mix(g)
                for g, n in at(s, MIX + 3):
                    feed(g)
                for g, n in at(s, MIX + 4):
                    feed_in(g)
                for g, n in at(s, EMBED + 2):
                    embed(g)
                for g, n in at(s, EMBED + 3):
                    project(g)
                for g, n in at(s, GELU):
                    importance(g)

        @block.gpsimd
        def _(pool):
            gp = nc.gpsimd
            mine = [0]

            def link(ins):
                mine[0] += 1
                ins.then_inc(own["pool"], 1)
                pool.wait_ge(own["pool"], mine[0])

            def normalise(g, c):
                if c == 0:
                    pool.wait_ge(var_ok, upto(var_ok, g))
                    gp.tensor_tensor(mom[:, g, 2:3], mom[:, g, 4:5], eps_col[:, 0:1], ALU.pow).then_inc(rstd_ok, 1)
                    pool.wait_ge(rstd_ok, upto(rstd_ok, g))
                pool.wait_ge(xt_tr, upto(xt_tr, g, (XROWS * c + XROWS - 1) // 4))
                v = X[g % 2][:, c * XROWS:(c + 1) * XROWS, :].rearrange("p r j -> p (r j)")
                gp.tensor_scalar(v, v, mom[:, g, 3:4], mom[:, g, 2:3], ALU.add, ALU.mult).then_inc(xn_ok, 1)

            def split(g, n):
                if n == 0:
                    pool.wait_ge(im_ok, upto(im_ok, g))
                    if g:
                        pool.wait_ge(parts_w, upto(parts_w, g - 1))
                if n < 2:
                    link(gp.tensor_copy(parts[:, n], im[:]))
                    link(gp.tensor_tensor(im[:], im[:], parts[:, n], ALU.subtract))
                else:
                    gp.tensor_copy(parts[:, 2], im[:]).then_inc(part_ok, 1)

            def gather(g, k):
                if k == 0:
                    pool.wait_ge(idx_ok, upto(idx_ok, g))
                    for i in range(4):
                        pool.wait_ge(tab_first[i], upto(tab_first[i], 0))
                    if g:
                        for i in range(2):
                            pool.wait_ge(tab_w[i], upto(tab_w[i], g - 1))
                    pool.wait_ge(imp_w, upto(imp_w, g))
                    if g:
                        pool.wait_ge(tok_ok, upto(tok_ok, g - 1))
                    if g >= 2:
                        pool.wait_ge(t2_ok, upto(t2_ok, g - 2))
                for dst, src, n in ((tok_x[:, g % 2, k, :], table[g % TABLES], 0), (tok_imp[:, k:k + 1], imp_flat[g % 2], 1),
                                    (tok_pos[:, k, :], pos, 2)):
                    gp.indirect_dma_start(dst, None, src, bass.IndirectOffsetOnAxis(ap=idx[:, g % 2, n, k:k + 1], axis=0)
                                          ).then_inc(tok_in, 16)

            def masked(g, j):
                b, pair = j // 4, j % 4
                if j == 0:
                    pool.wait_ge(qk_cp, upto(qk_cp, g, 0))
                if b:
                    pool.wait_ge(s_ok, upto(s_ok, g, 8 * (b - 1) + 4 + pair))
                for h in range(2 * pair, 2 * pair + 2):
                    last = gp.tensor_scalar(qm[:, h, :], q_t[:], head_mask[:, NH * b + h:NH * b + h + 1], 1.0, ALU.mult, ALU.mult)
                last.then_inc(qm_ok, 1)

            def finish(g, u):
                pool.wait_ge(res_ok, upto(res_ok, g, u))
                v = res[:, (U * g + u) % 3, 0:ROWS[u] * H]
                gp.tensor_scalar(v, v, 1.0, mom[:, g, 0:1], ALU.mult, ALU.add).then_inc(fin_ok, 1)

            def scatter(g, part):
                pool.wait_ge(t2_ok, upto(t2_ok, g))
                for k in range(2 * part, 2 * part + 2):
                    gp.indirect_dma_start(table[g % TABLES], bass.IndirectOffsetOnAxis(ap=idx[:, g % 2, 0, k:k + 1], axis=0),
                                          rb[:, k, :], None).then_inc(scat, 16)

            pool.wait_ge(ready, 16 * NL)
            pool.wait_ge(dve_set, upto(dve_set, 0))
            gp.tensor_tensor(bn[:, 7:8], bn[:, 7:8], eps_col[0:H, 0:1], ALU.pow).then_inc(bn_rstd, 1)
            power_in = eps_col[0:HALF, 0:1].broadcast_to([HALF, 8])
            for s in SLOTS:
                for g, n in at(s, SCORES, 16):
                    if n % 4 >= 2 and n < 14:
                        for pair in (2 * (n % 2), 2 * (n % 2) + 1):
                            masked(g, n // 4 * 4 + 4 + pair)
                for g, n in at(s, BACK, U):
                    finish(g, n)
                for g, n in at(s, MIX + 2):
                    pool.wait_ge(v1_ok, upto(v1_ok, g))
                    gp.tensor_tensor(rs[:, 2, :], rs[:, 1, :], power_in, ALU.pow).then_inc(r1_ok, 1)
                for g, n in at(s, MIX + 6):
                    pool.wait_ge(v2_ok, upto(v2_ok, g))
                    gp.tensor_tensor(rs[:, 2, :], rs[:, 1, :], power_in, ALU.pow).then_inc(r2_ok, 1)
                for g, n in at(s, EMBED + 3):
                    for j in range(4):
                        masked(g, j)
                for g, n in at(s, GATHER, 8):
                    gather(g, n)
                for g, n in at(s, SCATTER, 4):
                    scatter(g, n)
                for k in range(3):
                    for g, n in at(s, SPLIT[k]):
                        split(g, k)
                for c in range(XC):
                    for g, n in at(s, NORMAL[c]):
                        normalise(g, c)

        @block.vector
        def _(dve):
            v = nc.vector
            mine = [0]

            def post(ins):
                mine[0] += 1
                ins.then_inc(own["dve"], 1)

            def sync():
                dve.wait_ge(own["dve"], mine[0])

            def link(ins):
                post(ins)
                sync()

            def piece(g, n):
                if n >= 25:
                    return
                if n % 5 == 0:
                    dve.wait_ge(x_in[g % 2][n // 5], upto(x_in[g % 2][n // 5], g // 2))
                post(v.bn_stats(stats[:, n, :], X[g % 2][:].rearrange("p i j -> p (i j)")[:, n * FL:(n + 1) * FL]))

            def moments(g):
                sync()
                link(v.bn_aggr(mom[:, g, 0:2], stats[:].rearrange("p a b -> p (a b)")))
                link(v.tensor_scalar(mom[:, g, 3:4], mom[:, g, 0:1], -1.0, None, ALU.mult))
                v.tensor_scalar(mom[:, g, 4:5], mom[:, g, 1:2], EPS, None, ALU.add).then_inc(var_ok, 1)

            def count(g, k):
                if k == 0:
                    dve.wait_ge(flat_in, upto(flat_in, g))
                    link(v.memset(th[:, 0:1], 0.4375 + 0.5))
                v.tensor_scalar(junk, flat[:], th[:, 0:1], None, ALU.is_ge, ALU.add, accum_out=cnt[:]).then_inc(cnt_ok, 1)

            def refine(g, k):
                dve.wait_ge(cnt_sum, upto(cnt_sum, g, k))
                step = 2.0 ** -(k + 1)
                v.tensor_scalar(th[:, 1:2], tr[0:100, COUNT + k:COUNT + k + 1], K - 0.5, step, ALU.is_ge, ALU.mult).then_inc(small_rd, 1)
                dve.wait_ge(small_rd, upto(small_rd, g, k))
                if k < TOPK_STEPS - 2:
                    link(v.scalar_tensor_tensor(th[:, 0:1], th[:, 1:2], -step / 2, th[:, 0:1], op0=ALU.add, op1=ALU.add))
                elif k == TOPK_STEPS - 2:
                    link(v.scalar_tensor_tensor(th[:, 2:3], th[:, 1:2], -step, th[:, 0:1], op0=ALU.add, op1=ALU.add))
                    link(v.tensor_scalar(th[:, 0:1], th[:, 2:3], step / 2, None, ALU.add))
                else:
                    link(v.tensor_tensor(th[:, 3:4], th[:, 1:2], th[:, 2:3], ALU.add))

            def find_first(g):
                v.tensor_scalar(tsel[:], first_chunk, th[:, 3:4], None, ALU.mult).then_inc(tsel_ok, 1)

            def find_masks(g):
                dve.wait_ge(tb_ok, upto(tb_ok, g))
                v.tensor_copy(tb[:], tr[0:H, THR:THR + NB]).then_inc(small_rd, 1)
                dve.wait_ge(small_rd, upto(small_rd, g, TOPK_STEPS))
                dve.wait_ge(imp_in, upto(imp_in, g))
                if g:
                    dve.wait_ge(part_ok, upto(part_ok, g - 1))
                for b in range(NB):
                    post(v.tensor_scalar(gt[:, b], imp[:, b], tb[:, b:b + 1], None, ALU.is_gt))
                    post(v.tensor_scalar(eq[:, b], imp[:, b], tb[:, b:b + 1], None, ALU.is_equal))
                sync()
                for b in range(NB):
                    post(v.tensor_tensor_scan(cg[:, b], gt[:, b], zrow[:], 0.0, ALU.add, ALU.add))
                    post(v.tensor_tensor_scan(ce[:, b], eq[:, b], zrow[:], 0.0, ALU.add, ALU.add))
                sync()
                link(v.tensor_copy(tot[:, 0:NB], cg[:, :, H - 1]))
                v.tensor_copy(tot[:, NB:2 * NB], ce[:, :, H - 1]).then_inc(tot_ok, 1)

            def find_ranks(g):
                dve.wait_ge(off_ok, upto(off_ok, g))
                post(v.tensor_copy(off[:, 0:8], tr[0:H, OFFS:OFFS + 8]))
                v.tensor_scalar(off[:, 8:12], tr[0:H, TOTS:TOTS + 4], -1.0, float(K), ALU.mult, ALU.add).then_inc(small_rd, 1)
                dve.wait_ge(small_rd, upto(small_rd, g))
                for b in range(NB):
                    post(v.tensor_scalar(ce[:, b], ce[:, b], off[:, 4 + b:5 + b], off[:, 8 + b:9 + b], ALU.add, ALU.min))
                post(v.tensor_tensor(off[:, 12:16], off[:, 4:8], off[:, 8:12], ALU.min))
                sync()
                for b in range(NB):
                    post(v.scalar_tensor_tensor(cs[:, b, 0:H], cg[:, b], off[:, b:b + 1], ce[:, b], op0=ALU.add, op1=ALU.add))
                post(v.tensor_tensor(startend[:, 0:NB], off[:, 0:4], off[:, 12:16], ALU.add))
                sync()
                post(v.tensor_copy(startend[:, NB:2 * NB], cs[:, :, H - 1]))

            def find_hot(g):
                sync()
                for b in range(NB):
                    post(v.tensor_scalar(hot_a[:, b], iota_k, startend[:, b:b + 1], None, ALU.is_ge))
                sync()
                for b in range(NB - 1):
                    post(v.scalar_tensor_tensor(hot[:, b], iota_k, startend[:, NB + b:NB + b + 1], hot_a[:, b],
                                                op0=ALU.is_lt, op1=ALU.mult))
                v.scalar_tensor_tensor(hot[:, NB - 1], iota_k, startend[:, 2 * NB - 1:2 * NB], hot_a[:, NB - 1],
                                       op0=ALU.is_lt, op1=ALU.mult).then_inc(hot_ok, 1)

            def find_rest(g):
                post(v.tensor_tensor(gt[:, :, 1:H], cs[:, :, 1:H], cs[:, :, 0:H - 1], ALU.subtract))
                post(v.tensor_tensor(gt[:, :, 0], cs[:, :, 0], startend[:, 0:NB], ALU.subtract))
                sync()
                v.scalar_tensor_tensor(im[:].rearrange("p b j -> p (b j)"), gt[:].rearrange("p b j -> p (b j)"), 0.5,
                                       imp[:].rearrange("p b j -> p (b j)"), op0=ALU.is_lt, op1=ALU.mult).then_inc(im_ok, 1)

            def find_index(g, half):
                dve.wait_ge(pick_ok, upto(pick_ok, g))
                for b in range(NB):
                    k = NB * half + b
                    post(v.tensor_scalar(jcol[:, k], sc[0:HALF, half, 112 * b:112 * b + H], slot_col[:, half:half + 1], None,
                                         ALU.is_le, ALU.add, accum_out=col[:, k:k + 1]))
                if half == 0:
                    return
                sync()
                for half in range(2):
                    ks = slice(NB * half, NB * half + NB)
                    rows = sc[0:HALF, half, 0:448].rearrange("p (b j) -> p b j", j=112)[:, :, 110]
                    post(v.scalar_tensor_tensor(pixf[:, 2, ks], rows, float(H), col[:, ks], op0=ALU.mult, op1=ALU.add))
                    post(v.scalar_tensor_tensor(pixf[:, 0, ks], col[:, ks], float(H), rows, op0=ALU.mult, op1=ALU.add))
                sync()
                post(v.scalar_tensor_tensor(pixf[:, 0], pixf[:, 0], float(NB), tab_base, op0=ALU.mult, op1=ALU.add))
                post(v.tensor_tensor(pixf[:, 1], pixf[:, 2], imp_base, ALU.add))
                sync()
                if g >= 2:
                    dve.wait_ge(scat, upto(scat, g - 2))
                v.tensor_copy(idx[:, g % 2], pixf[:]).then_inc(idx_ok, 1)

            def importance_sum(g, n):
                if n == 0:
                    dve.wait_ge(y7_in, upto(y7_in, g))
                b = slice(2 * n, 2 * n + 2)
                v.reduce_sum(yy[:, b], y7[:, b].rearrange("p b k j -> p b j k"), AX).then_inc(y_ok, 1)

            def importance(g, n):
                if n == 0:
                    dve.wait_ge(gelu_ok, upto(gelu_ok, g))
                b = slice(2 * n, 2 * n + 2)
                link(v.tensor_scalar(yy[:, b], ge[:, b], 1.0, None, ALU.add))
                v.reciprocal(ge[:, b], yy[:, b]).then_inc(imp_ok, 1)

            def diagonals(g):
                post(v.tensor_scalar(diag[:, 0:128], ident, mom[:, g, 0:1], None, ALU.mult))
                v.tensor_scalar(diag[:, 128:256], ident, mom[:, g, 2:3], None, ALU.mult).then_inc(diag_ok, 1)

            def embed(g):
                dve.wait_ge(tok_in, upto(tok_in, g))
                dve.wait_ge(rep_ok, upto(rep_ok, g))
                m = pp[0:HALF, 0:128].rearrange("p (b c) -> p b c", c=C)
                r = pp[0:HALF, 128:256].rearrange("p (b c) -> p b c", c=C)
                for half in range(2):
                    ks = slice(NB * half, NB * half + NB)
                    post(v.tensor_tensor(tok[:, ks], tok_x[:, g % 2, ks], m, ALU.subtract))
                sync()
                for half in range(2):
                    ks = slice(NB * half, NB * half + NB)
                    post(v.tensor_tensor(tok[:, ks], tok[:, ks], r, ALU.mult))
                sync()
                link(v.tensor_tensor(tok[:], tok[:], tok_imp[:].unsqueeze(2).to_broadcast([HALF, 8, C]), ALU.mult))
                v.tensor_tensor(tok[:], tok[:], tok_pos[:], ALU.add).then_inc(tok_ok, 1)

            def value_rows(g):
                dve.wait_ge(qkv_ok, upto(qkv_ok, g))
                for half in range(2):
                    last = v.tensor_tensor(vpad[:, half, :, 0:HD],
                                           ms[0:HALF, 128 * half:128 * half + 128].rearrange("p (h d) -> p h d", d=HD),
                                           rep[:, 0].rearrange("p b (h d) -> p (b h) d", d=HD), ALU.add)
                    if half == 0:
                        post(last)
                last.then_inc(v_cp, 1)

            def least_of(g, k):
                dve.wait_ge(s_ok, upto(s_ok, g, k))
                if k >= 2:
                    dve.wait_ge(e_ok, upto(e_ok, g, k - 2))
                elif g:
                    dve.wait_ge(e_ok, upto(e_ok, g - 1))
                v.tensor_reduce(least[:, k % 2], sc[0:HALF, k % 2, 0:2 * K].rearrange("p (h q) -> p h q", q=K),
                                AX, ALU.min).then_inc(least_ok, 1)

            def values(g, unit):
                b, half = unit // 2, unit % 2
                dve.wait_ge(ot_tr, upto(ot_tr, g, unit))
                o = ms[0:HALF, 256:512].rearrange("p (h d) -> p h d", d=32)
                link(v.reciprocal(rden[:].rearrange("p a h -> p (a h)"), o[:, :, HD]))
                v.tensor_tensor(o_tok[:, half, b].rearrange("p (h d) -> p h d", d=HD), o[:, :, 0:HD],
                                rden[:].rearrange("p a h -> p (a h)").unsqueeze(2).to_broadcast([HALF, NH, HD]),
                                ALU.mult).then_inc(o_ok, 1)

            halves = slice(0, NB), slice(NB, 2 * NB)

            def norm_first(y, bias, res_in, out_v):
                for half in range(2):
                    post(v.tensor_tensor(out_v[:, halves[half]], y[:, halves[half]], rep[:, bias], ALU.add))
                sync()
                link(v.tensor_tensor(out_v[:], out_v[:], res_in[:], ALU.add))
                link(v.reduce_sum(rs[:, 0, :], out_v[:], AX))
                link(v.tensor_scalar(rs[:, 0, :], rs[:, 0, :], 1.0 / C, None, ALU.mult))
                link(v.tensor_tensor(out_v[:], out_v[:], rs[:, 0, :].unsqueeze(2).to_broadcast([HALF, 8, C]), ALU.subtract))
                link(v.tensor_tensor(sq, out_v[:], out_v[:], ALU.mult))
                link(v.reduce_sum(rs[:, 3, :], sq, AX))
                return v.tensor_scalar(rs[:, 1, :], rs[:, 3, :], 1.0 / C, EPS, ALU.mult, ALU.add)

            def norm_last(gain, shift, out_v):
                link(v.tensor_tensor(out_v[:], out_v[:], rs[:, 2, :].unsqueeze(2).to_broadcast([HALF, 8, C]), ALU.mult))
                for half in range(2):
                    post(v.tensor_tensor(out_v[:, halves[half]], out_v[:, halves[half]], rep[:, gain], ALU.mult))
                sync()
                post(v.tensor_tensor(out_v[:, halves[0]], out_v[:, halves[0]], rep[:, shift], ALU.add))
                return v.tensor_tensor(out_v[:, halves[1]], out_v[:, halves[1]], rep[:, shift], ALU.add)

            def unit_back(g, u):
                dve.wait_ge(rt_tr, upto(rt_tr, g, u))
                dve.wait_ge(wgt_ok, upto(wgt_ok, g, u))
                place = (U * g + u) % 3
                if U * g + u >= 3:
                    dve.wait_ge(out_w[place], 16 * ((U * g + u) // 3))
                n = ROWS[u] * H
                v.scalar_tensor_tensor(res[:, place, 0:n], back_bank(g, u)[:, 0:n], mom[:, g, 0:1], wgt[:, 0:n],
                                       op0=ALU.subtract, op1=ALU.mult).then_inc(res_ok, 1)

            for w in (ms, w_conv, wq, wk, wv, wo, w1, w2, y7, vpad, zrow, cvr):
                post(v.memset(w[:], 0.0))
            post(v.memset(eps_col[:, 0:1], -0.5))
            post(v.memset(eps_col[:, 1:2], 1.0))
            sync()
            v.memset(vpad[:, :, :, HD:HD + 1], 1.0).then_inc(dve_set, 1)
            for n in range(25):
                piece(0, n)
            moments(0)
            dve.wait_ge(cst_in, upto(cst_in, 0))
            dve.wait_ge(ready, 16 * NL)
            for b in range(NB):
                q = slice(C * b, C * b + C)
                post(v.tensor_copy(w_conv[q, :, KS * b:KS * b + KS], w_small[q]))
            post(v.tensor_copy(blk[:], blk_f))
            post(v.tensor_copy(bones[:], bones_f))
            for b in range(NB):
                post(v.tensor_copy(cs[:, b, 110:111], row_col))
            link(v.tensor_scalar(bn[:, 7:8], bn[:, 4:5], EPS, None, ALU.add))
            link(v.tensor_scalar(bn[:, 6:7], bn[:, 0:1], bn[:, 3:4], None, ALU.subtract))
            v.memset(rs[:], 0.0).then_inc(dve_set, 1)
            dve.wait_ge(bn_rstd, upto(bn_rstd, 0))
            link(v.tensor_tensor(bn[:, 5:6], bn[:, 1:2], bn[:, 7:8], ALU.mult))
            link(v.tensor_scalar(bn[:, 6:7], bn[:, 6:7], bn[:, 5:6], bn[:, 2:3], ALU.mult, ALU.add))
            for s in SLOTS:
                for g, n in at(s, SEARCH, TOPK_STEPS):
                    count(g, n)
                for g, n in at(s, BACK, U):
                    unit_back(g, n)
                for g, n in at(s, SCORES, 16):
                    least_of(g, 2 * n)
                for g, n in at(s, SCORES, 16):
                    least_of(g, 2 * n + 1)
                for g, n in at(s, SEARCH, TOPK_STEPS):
                    refine(g, n)
                for g, n in at(s, INTO, U):
                    if g:
                        piece(g, n)
                for g, n in at(s, VALUES, 16):
                    if n % 2:
                        values(g, n // 2)
                for g, n in at(s, SUM, 2):
                    importance_sum(g, n)
                for g, n in at(s, GELU + 2, 2):
                    importance(g, n)
                for g, n in at(s, MASKS - 1):
                    find_first(g)
                for g, n in at(s, MASKS):
                    find_masks(g)
                for g, n in at(s, RANKS):
                    find_ranks(g)
                for g, n in at(s, RANKS + 1):
                    find_hot(g)
                for g, n in at(s, INDEX, 2):
                    find_index(g, n)
                for g, n in at(s, REST):
                    find_rest(g)
                y = ms[0:HALF, 0:256].rearrange("p (k c) -> p k c", c=C)
                for g, n in at(s, EMBED):
                    diagonals(g)
                for g, n in at(s, EMBED + 1):
                    embed(g)
                for g, n in at(s, EMBED + 3):
                    value_rows(g)
                for g, n in at(s, MIX + 1):
                    dve.wait_ge(wo_ok, upto(wo_ok, g))
                    norm_first(y, 1, tok, ra).then_inc(v1_ok, 1)
                for g, n in at(s, MIX + 2):
                    dve.wait_ge(r1_ok, upto(r1_ok, g))
                    norm_last(2, 3, ra).then_inc(t1_ok, 1)
                for g, n in at(s, MIX + 5):
                    dve.wait_ge(ff_ok, upto(ff_ok, g))
                    norm_first(y, 4, ra, rb).then_inc(v2_ok, 1)
                for g, n in at(s, MIX + 6):
                    dve.wait_ge(r2_ok, upto(r2_ok, g))
                    link(norm_last(5, 6, rb))
                    v.tensor_tensor(rb[:], rb[:], tok_x[:, g % 2], ALU.add).then_inc(t2_ok, 1)
                for g, n in at(s, INTO + U - 1):
                    if g:
                        moments(g)


def constants(H, C, NB, NH, K):
    import numpy as np

    def wide(a):
        a = np.asarray(a, np.float32)
        return np.concatenate([a, np.zeros((128 - a.shape[0], a.shape[1]), np.float32)])

    p = np.arange(128)
    rows = np.arange(H)
    c100 = np.arange(100)
    slots = np.arange(96)
    return np.concatenate([wide(a) for a in (
        np.eye(128), np.ones((128, 128)), rows[:, None] < rows[None, :], c100[:, None] // 25 == c100[None, :] // 25,
        (p[:, None] // (C // NH)) == np.arange(NB * NH)[None, :], np.tile(np.arange(K), (H, 1)),
        np.stack([slots, slots + 96], 1), rows[:, None], c100[:, None] == 25 * np.arange(NB)[None, :],
        np.tile(np.tile(np.arange(NB), 2), (96, 1)), np.tile(np.tile(np.arange(NB), 2) * H * H, (96, 1)),
        np.arange(12)[:, None] % NB == p[None, :] // C,
    )], axis=1).astype(np.float32)


def positions(seq_len, dim):
    import numpy as np
    pos = np.arange(seq_len, dtype=np.float32)[:, None]
    div = np.exp(np.arange(0, dim, 2, dtype=np.float32) * -(np.log(10000.0) / dim))
    pe = np.zeros((seq_len, dim), dtype=np.float32)
    pe[:, 0::2] = np.sin(pos * div)
    pe[:, 1::2] = np.cos(pos * div)
    return pe


def kernel(**inputs):
    import numpy as np
    import concourse.bacc as bacc
    from concourse import mybir
    from concourse.bass_utils import run_bass_kernel_spmd

    a = {k.removeprefix("L0_conv_"): np.asarray(v) for k, v in inputs.items()}
    B, C, H, _ = a["x"].shape
    arrays = {
        "in_x": a["x"],
        "in_conv_w": a["conv_w"][0].transpose(0, 2, 1),
        "in_conv_b": a["conv_b"], "in_bn_g": a["bn_g"], "in_bn_b": a["bn_b"], "in_bn_m": a["bn_m"], "in_bn_v": a["bn_v"],
        "in_w_qkvT": a["w_qkv"].T, "in_b_qkv": a["b_qkv"], "in_w_oT": a["w_o"].T, "in_b_o": a["b_o"],
        "in_ln1_g": a["ln1_g"], "in_ln1_b": a["ln1_b"], "in_w1T": a["w1"].T, "in_b1": a["b1"],
        "in_w2T": a["w2"].T, "in_b2": a["b2"], "in_ln2_g": a["ln2_g"], "in_ln2_b": a["ln2_b"],
        "in_pos": positions(H * H, C), "in_const": constants(H, C, 128 // C, 8, 192),
    }
    arrays = {k: np.ascontiguousarray(v) for k, v in arrays.items()}
    nc = bacc.Bacc("TRN2", target_bir_lowering=False, num_devices=1)
    args = [nc.dram_tensor(k, v.shape, mybir.dt.from_np(v.dtype), kind="ExternalInput").ap() for k, v in arrays.items()]
    out = nc.dram_tensor("out", a["x"].shape, mybir.dt.float32, kind="ExternalOutput").ap()
    preact_conv_token_attention(nc, *args, out)
    r = run_bass_kernel_spmd(nc, [arrays], core_ids=[0])
    return r.results[0]["out"]
```
